# Optimizing a Trainium2 kernel written in Bass

```python
import numpy as np
import jax
import jax.numpy as jnp

def _softmax(x, axis=-1):
    return jax.nn.softmax(x, axis=axis)
def _gelu(x):
    return jax.nn.gelu(x, approximate=True)
def _silu(x):
    return jax.nn.silu(x)
def _sigmoid(x):
    return jax.nn.sigmoid(x)
def _layernorm(x, axis=-1, eps=1e-5):
    m = jnp.mean(x, axis=axis, keepdims=True)
    v = jnp.var(x, axis=axis, keepdims=True)
    return (x - m) / jnp.sqrt(v + eps)
def _scatter_add(tgt, idx, src, axis=0):
    return tgt.at[idx].add(src)
def _segment_sum(src, seg, n):
    return jax.ops.segment_sum(src, seg, n)

kernel_name = 'mk_conv_attn_hybrid_d2_conv_nchw384_bd3b13'

def setup_inputs(seed: int = 0):
    np.random.seed(seed)
    _w = jnp.asarray
    def _rec_inputs():
        import jax
        import jax.numpy as jnp
        _gk = jax.random.key(seed)
        x = -0.0005963 + 1.001 * jax.random.normal(jax.random.fold_in(_gk, 1), (8, 384, 32, 32), jnp.float32)
        return x
    x = _rec_inputs()
    def _L0_conv_setup():
        import jax, jax.numpy as jnp
        import numpy as np
        D_STATE = 16
        D_CONV = 4

        def rmsnorm(x, w, eps=1e-06):
            return x * jax.lax.rsqrt(jnp.mean(x * x, axis=-1, keepdims=True) + eps) * w

        def silu(x):
            return x * jax.nn.sigmoid(x)

        def mamba(x, in_proj_w, conv1d_w, conv1d_b, x_proj_w, dt_proj_w, dt_proj_b, A_log, D_param, out_proj_w):
            B, L, C = x.shape
            dt_rank = dt_proj_w.shape[1]
            xz = jnp.einsum('blc,ec->ble', x, in_proj_w)
            u, z = jnp.split(xz, 2, axis=-1)
            uc = jax.lax.conv_general_dilated(u.transpose(0, 2, 1), conv1d_w[:, None, :], (1,), [(D_CONV - 1, 0)], dimension_numbers=('NCH', 'OIH', 'NCH'), feature_group_count=C)
            u = silu((uc + conv1d_b[None, :, None]).transpose(0, 2, 1))
            x_dbl = jnp.einsum('blc,ec->ble', u, x_proj_w)
            dt, Bm, Cm = jnp.split(x_dbl, [dt_rank, dt_rank + D_STATE], axis=-1)
            delta = jax.nn.softplus(jnp.einsum('blr,dr->bld', dt, dt_proj_w) + dt_proj_b)
            A = -jnp.exp(A_log)
            deltaA = jnp.exp(delta[..., None] * A)
            deltaBu = (delta * u)[..., None] * Bm[:, :, None, :]

            def step(h, inp):
                dA, dBu, c = inp
                h = dA * h + dBu
                return (h, jnp.einsum('bdn,bn->bd', h, c))
            h0 = jnp.zeros((B, C, D_STATE), x.dtype)
            _, ys = jax.lax.scan(step, h0, (deltaA.transpose(1, 0, 2, 3), deltaBu.transpose(1, 0, 2, 3), Cm.transpose(1, 0, 2)))
            y = ys.transpose(1, 0, 2) + u * D_param
            y = y * silu(z)
            return jnp.einsum('bld,od->blo', y, out_proj_w)
        key = jax.random.key(seed)
        ks = jax.random.split(key, 10)
        B, C, H, W = (8, 384, 32, 32)
        dt_rank = 24
        s = 0.02
        f32 = jnp.float32
        return {'x': jax.random.normal(ks[0], (B, C, H, W), f32), 'norm_w': jnp.ones((C,), f32), 'in_proj_w': jax.random.normal(ks[1], (2 * C, C), f32) * s, 'conv1d_w': jax.random.normal(ks[2], (C, D_CONV), f32) * 0.2, 'conv1d_b': jnp.zeros((C,), f32), 'x_proj_w': jax.random.normal(ks[3], (dt_rank + 2 * D_STATE, C), f32) * s, 'dt_proj_w': jax.random.normal(ks[4], (C, dt_rank), f32) * 0.1, 'dt_proj_b': jax.random.uniform(ks[5], (C,), f32, -4.0, -2.0), 'A_log': jnp.log(jnp.tile(jnp.arange(1, D_STATE + 1, dtype=f32), (C, 1))), 'D_param': jnp.ones((C,), f32), 'out_proj_w': jax.random.normal(ks[6], (C, C), f32) * s, 'scale_mod': jnp.full((1,), 0.25, f32), 'dw_w': jax.random.normal(ks[7], (C, 3, 3), f32) * 0.1, 'dw_b': jnp.zeros((C,), f32), 'res_scale': jnp.full((1,), 0.5, f32)}
    _L0_conv_all = _L0_conv_setup()
    _L0_conv_in = {k: v for k, v in _L0_conv_all.items() if k in ('norm_w', 'in_proj_w', 'conv1d_w', 'conv1d_b', 'x_proj_w', 'dt_proj_w', 'dt_proj_b', 'A_log', 'D_param', 'out_proj_w', 'scale_mod', 'dw_w', 'dw_b', 'res_scale', )}
    del _L0_conv_all

    def _L1_attn_setup():
        import jax, jax.numpy as jnp
        import numpy as np
        B, T, C = (4, 2048, 384)
        NUM_HEADS, HEAD_SIZE = (6, 64)
        key = jax.random.key(seed)
        ks = jax.random.split(key, 6)
        s = 1.0 / np.sqrt(C)
        return {'x': jax.random.normal(ks[0], (B, T, C), dtype=jnp.float32), 'Wq': jax.random.normal(ks[1], (C, NUM_HEADS * HEAD_SIZE), dtype=jnp.float32) * s, 'bq': jnp.zeros((NUM_HEADS * HEAD_SIZE,), dtype=jnp.float32), 'Wk': jax.random.normal(ks[2], (C, NUM_HEADS * HEAD_SIZE), dtype=jnp.float32) * s, 'bk': jnp.zeros((NUM_HEADS * HEAD_SIZE,), dtype=jnp.float32), 'Wv': jax.random.normal(ks[3], (C, NUM_HEADS * HEAD_SIZE), dtype=jnp.float32) * s, 'bv': jnp.zeros((NUM_HEADS * HEAD_SIZE,), dtype=jnp.float32), 'Wo': jax.random.normal(ks[4], (NUM_HEADS * HEAD_SIZE, C), dtype=jnp.float32) * s, 'bo': jnp.zeros((C,), dtype=jnp.float32)}
    _L1_attn_all = _L1_attn_setup()
    _L1_attn_in = {k: v for k, v in _L1_attn_all.items() if k in ('Wq', 'bq', 'Wk', 'bk', 'Wv', 'bv', 'Wo', 'bo', )}
    del _L1_attn_all

    def _L1_ffn_setup():
        import jax, jax.numpy as jnp
        import numpy as np
        D_MODEL = 384
        D_FF = 1536
        key = jax.random.key(seed)
        k_x, k1, k2, k3, k4 = jax.random.split(key, 5)
        std = 0.02
        return {'x': jax.random.normal(k_x, (16, 2048, D_MODEL), dtype=jnp.float32), 'c_fc_1': std * jax.random.normal(k1, (1536, 32), dtype=jnp.float32), 'c_fc_2': std * jax.random.normal(k2, (1, 12), dtype=jnp.float32), 'c_proj_1': std * jax.random.normal(k3, (32, 1536), dtype=jnp.float32), 'c_proj_2': std * jax.random.normal(k4, (12, 1), dtype=jnp.float32)}
    _L1_ffn_all = _L1_ffn_setup()
    _L1_ffn_in = {k: v for k, v in _L1_ffn_all.items() if k in ('c_fc_1', 'c_fc_2', 'c_proj_1', 'c_proj_2', )}
    del _L1_ffn_all

    return {
        "x": x,
        "L0_conv_norm_w": _L0_conv_in["norm_w"],
        "L0_conv_in_proj_w": _L0_conv_in["in_proj_w"],
        "L0_conv_conv1d_w": _L0_conv_in["conv1d_w"],
        "L0_conv_conv1d_b": _L0_conv_in["conv1d_b"],
        "L0_conv_x_proj_w": _L0_conv_in["x_proj_w"],
        "L0_conv_dt_proj_w": _L0_conv_in["dt_proj_w"],
        "L0_conv_dt_proj_b": _L0_conv_in["dt_proj_b"],
        "L0_conv_A_log": _L0_conv_in["A_log"],
        "L0_conv_D_param": _L0_conv_in["D_param"],
        "L0_conv_out_proj_w": _L0_conv_in["out_proj_w"],
        "L0_conv_scale_mod": _L0_conv_in["scale_mod"],
        "L0_conv_dw_w": _L0_conv_in["dw_w"],
        "L0_conv_dw_b": _L0_conv_in["dw_b"],
        "L0_conv_res_scale": _L0_conv_in["res_scale"],
        "L1_attn_Wq": _L1_attn_in["Wq"],
        "L1_attn_bq": _L1_attn_in["bq"],
        "L1_attn_Wk": _L1_attn_in["Wk"],
        "L1_attn_bk": _L1_attn_in["bk"],
        "L1_attn_Wv": _L1_attn_in["Wv"],
        "L1_attn_bv": _L1_attn_in["bv"],
        "L1_attn_Wo": _L1_attn_in["Wo"],
        "L1_attn_bo": _L1_attn_in["bo"],
        "L1_ffn_c_fc_1": _L1_ffn_in["c_fc_1"],
        "L1_ffn_c_fc_2": _L1_ffn_in["c_fc_2"],
        "L1_ffn_c_proj_1": _L1_ffn_in["c_proj_1"],
        "L1_ffn_c_proj_2": _L1_ffn_in["c_proj_2"],
    }

def reference(x, L0_conv_norm_w, L0_conv_in_proj_w, L0_conv_conv1d_w, L0_conv_conv1d_b, L0_conv_x_proj_w, L0_conv_dt_proj_w, L0_conv_dt_proj_b, L0_conv_A_log, L0_conv_D_param, L0_conv_out_proj_w, L0_conv_scale_mod, L0_conv_dw_w, L0_conv_dw_b, L0_conv_res_scale, L1_attn_Wq, L1_attn_bq, L1_attn_Wk, L1_attn_bk, L1_attn_Wv, L1_attn_bv, L1_attn_Wo, L1_attn_bo, L1_ffn_c_fc_1, L1_ffn_c_fc_2, L1_ffn_c_proj_1, L1_ffn_c_proj_2):
    import jax
    import jax.numpy as jnp
    def _L0_conv_ref(x, norm_w, in_proj_w, conv1d_w, conv1d_b, x_proj_w, dt_proj_w, dt_proj_b, A_log, D_param, out_proj_w, scale_mod, dw_w, dw_b, res_scale):
        import jax, jax.numpy as jnp
        import numpy as np
        D_STATE = 16
        D_CONV = 4

        def rmsnorm(x, w, eps=1e-06):
            return x * jax.lax.rsqrt(jnp.mean(x * x, axis=-1, keepdims=True) + eps) * w

        def silu(x):
            return x * jax.nn.sigmoid(x)

        def mamba(x, in_proj_w, conv1d_w, conv1d_b, x_proj_w, dt_proj_w, dt_proj_b, A_log, D_param, out_proj_w):
            B, L, C = x.shape
            dt_rank = dt_proj_w.shape[1]
            xz = jnp.einsum('blc,ec->ble', x, in_proj_w)
            u, z = jnp.split(xz, 2, axis=-1)
            uc = jax.lax.conv_general_dilated(u.transpose(0, 2, 1), conv1d_w[:, None, :], (1,), [(D_CONV - 1, 0)], dimension_numbers=('NCH', 'OIH', 'NCH'), feature_group_count=C)
            u = silu((uc + conv1d_b[None, :, None]).transpose(0, 2, 1))
            x_dbl = jnp.einsum('blc,ec->ble', u, x_proj_w)
            dt, Bm, Cm = jnp.split(x_dbl, [dt_rank, dt_rank + D_STATE], axis=-1)
            delta = jax.nn.softplus(jnp.einsum('blr,dr->bld', dt, dt_proj_w) + dt_proj_b)
            A = -jnp.exp(A_log)
            deltaA = jnp.exp(delta[..., None] * A)
            deltaBu = (delta * u)[..., None] * Bm[:, :, None, :]

            def step(h, inp):
                dA, dBu, c = inp
                h = dA * h + dBu
                return (h, jnp.einsum('bdn,bn->bd', h, c))
            h0 = jnp.zeros((B, C, D_STATE), x.dtype)
            _, ys = jax.lax.scan(step, h0, (deltaA.transpose(1, 0, 2, 3), deltaBu.transpose(1, 0, 2, 3), Cm.transpose(1, 0, 2)))
            y = ys.transpose(1, 0, 2) + u * D_param
            y = y * silu(z)
            return jnp.einsum('bld,od->blo', y, out_proj_w)
        B, C, H, W = x.shape
        x_cl = x.transpose(0, 2, 3, 1)
        xn_cl = rmsnorm(x_cl, norm_w)
        x_norm = xn_cl.transpose(0, 3, 1, 2)
        x_flat = xn_cl.reshape(B, H * W, C)
        mparams = (in_proj_w, conv1d_w, conv1d_b, x_proj_w, dt_proj_w, dt_proj_b, A_log, D_param, out_proj_w)
        fwd = mamba(x_flat, *mparams)
        bwd = jnp.flip(mamba(jnp.flip(x_flat, axis=1), *mparams), axis=1)
        g = (fwd + bwd) * scale_mod
        global_feat = g.reshape(B, H, W, C).transpose(0, 3, 1, 2)
        conv = jax.lax.conv_general_dilated(x_norm, dw_w[:, None, :, :], (1, 1), [(1, 1), (1, 1)], dimension_numbers=('NCHW', 'OIHW', 'NCHW'), feature_group_count=C)
        local_feat = jax.nn.sigmoid(conv + dw_b[None, :, None, None]) * x_norm
        return x + res_scale * (global_feat + local_feat)

    def _L1_attn_ref(x, Wq, bq, Wk, bk, Wv, bv, Wo, bo):
        import jax, jax.numpy as jnp
        import numpy as np
        B, T, C = (4, 2048, 384)
        NUM_HEADS, HEAD_SIZE = (6, 64)
        b, t, c = x.shape
        h, d = (NUM_HEADS, HEAD_SIZE)
        q = (x @ Wq + bq).reshape(b, t, h, d)
        k = (x @ Wk + bk).reshape(b, t, h, d)
        v = (x @ Wv + bv).reshape(b, t, h, d)
        scores = jnp.einsum('bthd,bshd->bhts', q, k) / jnp.sqrt(jnp.float32(d))
        causal = jnp.tril(jnp.ones((t, t), dtype=bool))
        scores = jnp.where(causal, scores, -jnp.inf)
        weights = jax.nn.softmax(scores, axis=-1)
        ctx = jnp.einsum('bhts,bshd->bthd', weights, v).reshape(b, t, h * d)
        return ctx @ Wo + bo

    def _L1_ffn_ref(x, c_fc_1, c_fc_2, c_proj_1, c_proj_2):
        import jax, jax.numpy as jnp
        import numpy as np
        D_MODEL = 384
        D_FF = 1536
        w_fc = jnp.kron(c_fc_1, c_fc_2)
        w_proj = jnp.kron(c_proj_1, c_proj_2)
        h = x @ w_fc.T
        h = jax.nn.gelu(h, approximate=False)
        out = h @ w_proj.T
        return out

    def _gn(v, G=32, eps=1e-5):
        B_, C_, H_, W_ = v.shape
        g = v.reshape(B_, G, C_ // G, H_, W_)
        m = jnp.mean(g, axis=(2, 3, 4), keepdims=True)
        s = jnp.var(g, axis=(2, 3, 4), keepdims=True)
        return ((g - m) / jnp.sqrt(s + eps)).reshape(v.shape)

    def _ln_c(v, eps=1e-6):
        m = jnp.mean(v, axis=1, keepdims=True)
        s = jnp.var(v, axis=1, keepdims=True)
        return (v - m) / jnp.sqrt(s + eps)

    def _ln_t(v, eps=1e-5):
        m = jnp.mean(v, axis=-1, keepdims=True)
        s = jnp.var(v, axis=-1, keepdims=True)
        return (v - m) / jnp.sqrt(s + eps)

    def _to_tokens(v):
        B_, C_, H_, W_ = v.shape
        return v.reshape(B_, C_, H_ * W_).transpose(0, 2, 1)
    def _from_tokens(t, like):
        B_, C_, H_, W_ = like.shape
        return t.transpose(0, 2, 1).reshape(B_, C_, H_, W_)

    x = _L0_conv_ref(x, L0_conv_norm_w, L0_conv_in_proj_w, L0_conv_conv1d_w, L0_conv_conv1d_b, L0_conv_x_proj_w, L0_conv_dt_proj_w, L0_conv_dt_proj_b, L0_conv_A_log, L0_conv_D_param, L0_conv_out_proj_w, L0_conv_scale_mod, L0_conv_dw_w, L0_conv_dw_b, L0_conv_res_scale)
    t = _to_tokens(x)
    t = t + _L1_attn_ref(_ln_t(t), L1_attn_Wq, L1_attn_bq, L1_attn_Wk, L1_attn_bk, L1_attn_Wv, L1_attn_bv, L1_attn_Wo, L1_attn_bo)
    t = t + _L1_ffn_ref(_ln_t(t), L1_ffn_c_fc_1, L1_ffn_c_fc_2, L1_ffn_c_proj_1, L1_ffn_c_proj_2)
    x = _from_tokens(t, x)
    return x


_drawn_inputs = setup_inputs


def setup_inputs(seed=0):
    import zlib

    import numpy as np

    out = dict(_drawn_inputs(seed))
    spreads = {'L0_conv_norm_w': (1.0, 0.2),
     'L0_conv_conv1d_b': (0.0, 0.1),
     'L0_conv_D_param': (1.0, 0.2),
     'L0_conv_dw_b': (0.0, 0.1),
     'L1_attn_bq': (0.0, 0.1),
     'L1_attn_bk': (0.0, 0.1),
     'L1_attn_bv': (0.0, 0.1),
     'L1_attn_bo': (0.0, 0.1)}
    factors = {}
    for name, (base, spread) in spreads.items():
        noise = np.random.default_rng([zlib.crc32(name.encode()), seed]).standard_normal(out[name].shape)
        drawn = base * np.exp(spread * noise) if base else spread * noise
        out[name] = jnp.asarray(drawn.astype(out[name].dtype))
    for name, factor in factors.items():
        out[name] = (out[name] * factor).astype(out[name].dtype)
    return out
```

```python
from contextlib import ExitStack

import concourse.bass as bass
from concourse import mybir

F32 = mybir.dt.float32
BF16 = mybir.dt.bfloat16
ALU = mybir.AluOpType
ACT = mybir.ActivationFunctionType
AX = mybir.AxisListType.X

NB, C, HH, WW = 8, 384, 32, 32
L = HH * WW
KT = C // 128
HALF = L // 2
NS = 16
NTAP = 4
RANK = 24
NH, DH = 6, 64
QT = L // 128
FF = 1536
NF = FF // 128
KI = 32
WP = WW + 2
UP = L + 2 * (NTAP - 1)
ROWS = 2 * NS * KT
DROWS = NS * KT

(V_NW, V_CB, V_DTB, V_D, V_DWB, V_BQ, V_BK, V_BV, V_BO) = range(9)
V_CW, V_DW, V_A = 9, 13, 22
NV = V_A + NS

TILES = [(h, i) for h in range(NH) for i in (7, 0, 6, 1, 5, 2, 4, 3)]
NT = len(TILES)
GROUPS = []
FIRST_GROUP = []
for _s, (_h, _i) in enumerate(TILES):
    FIRST_GROUP.append(len(GROUPS))
    for _k in range(0, _i + 1, 4):
        GROUPS.append((_s, _k, min(4, _i + 1 - _k)))
FIRST_GROUP.append(len(GROUPS))
NG = len(GROUPS)

NPJ = 20
FGRP = 3
NFG = NF // FGRP
ITEMS = (
    [("ln_mean", 0, 0.8), ("ln_var", 0, 0.9), ("ln_scale", 0, 0.9)]
    + [("proj", t, 0.75) for t in range(NPJ)]
    + [("attend", p, 1.0) for p in range(NT + 2)]
    + [("ctx_t", g, 0.4) for g in range(6)]
    + [("wo", t, 0.75) for t in range(6)]
    + [("ln_mean", 1, 0.8), ("ln_var", 1, 0.9), ("ln_scale", 1, 0.9), ("mlp_in", 0, 1.5)]
    + [x for c in range(2) for x in [("mlp", c * (NFG + 1) + q, 1.4) for q in range(NFG + 1)] + [("mlp_out", c, 1.0)]]
)


def slots():
    total = sum(w for _, _, w in ITEMS)
    out, at = [[] for _ in range(ROWS)], 0.0
    for kind, n, w in ITEMS:
        out[min(ROWS - 1, int(at * ROWS / total))].append((kind, n))
        at += w
    return out


SLOTS = slots()


def hybrid_block(nc, x, chan, scal, k128, k32, w_in, w_x, w_dt, w_out, wq, wk, wv, wo, fc1, fc2, pr1, pr2, out):
    with ExitStack() as ctx:
        def sb(name, shape, dt=F32):
            return ctx.enter_context(nc.sbuf_tensor(name, shape, dt))

        def sem(name):
            return ctx.enter_context(nc.semaphore(name))

        vec = sb("vec", [128, KT, NV])
        consts = sb("consts", [128, 512])
        ident, ones_c = consts[:, 0:128], consts[:, 256:384]
        sel_bf = sb("sel_bf", [128, 32], BF16)
        ident_bf = sb("ident_bf", [128, 128], BF16)
        causal_bf = sb("causal_bf", [128, 128], BF16)
        tiny = sb("tiny", [128, 8])
        rs_col, g_col, eps6, eps5, bq_s = tiny[:, 0:1], tiny[:, 1:2], tiny[:, 2:3], tiny[:, 3:4], tiny[:, 4:7]
        xp_w = sb("xp_w", [128, KT, 56])
        op_w = sb("op_w", [128, KT, C])
        q_w, k_w, v_w, o_w = (sb(n, [128, KT, C]) for n in ("q_w", "k_w", "v_w", "o_w"))
        mixed = sb("mixed", [128, FF])
        fc_w = mixed[0:KI, :]
        dt_w = [mixed[32:32 + RANK, 0:C], mixed[96:96 + RANK, 0:C]]
        kout_w = mixed[64:64 + KI, 0:C]
        pr_w = sb("pr_w", [128, NF, KI])
        kin_w = sb("kin_w", [128, KT, KI])
        small = sb("small", [128, 64])
        stat = sb("stat", [128, 4, 2])

        xres = sb("xres", [128, KT, L])
        delta = sb("delta", [128, KT, L])
        du_f = sb("du_f", [128, KT, L])
        uc_b = sb("uc_b", [128, KT, L])
        y = sb("y", [128, KT, L])
        zs = sb("zs", [128, KT, L])
        dA = [sb(f"dA{i}", [128, L]) for i in range(2)]
        hb = [sb(f"hb{i}", [128, L]) for i in range(3)]
        bc3 = [sb(f"bc3_{d}", [96, L], BF16) for d in range(2)]
        narrow = sb("narrow", [128, L])
        xr = narrow[0:KI, :]
        dtr = [narrow[32:32 + RANK, :], narrow[96:96 + RANK, :]]
        rr = narrow[64:64 + KI, :]

        xa = sb("xa", [128, KT, L])
        xn_area = sb("xn_area", [128, KT * L])
        area0 = sb("area0", [128, KT * HH * WP + KT * 2 * WP])
        area1 = sb("area1", [128, KT * UP])
        area2 = sb("area2", [128, KT * L])
        prob = sb("prob", [128, L])
        pt = sb("pt", [128, 2, 512])

        def tiled(area):
            return area[:, 0:KT * L].rearrange("p (k t) -> p k t", k=KT)

        ip_w = xn_area[:, 0:KT * 2 * C].rearrange("p (k e) -> p k e", k=KT)
        xnp = area0[:, :].rearrange("p (k h w) -> p k h w", k=KT, h=HH + 2)
        up = area1[:, :].rearrange("p (k t) -> p k t", k=KT)
        uc_f = tiled(area2)
        uc = [uc_f, uc_b]
        du = [du_f, uc_b]
        xn1, xn2 = tiled(xn_area), tiled(area1)
        sq_of = [tiled(area0), tiled(area2)]
        lnx_of = [xn1, xn2]
        qT, kT, ctxT = tiled(area0), tiled(area1), tiled(area0)
        vtok = area2[:, :].rearrange("p (j c) -> p j c", j=QT)
        ctxk = xn_area[:, :].rearrange("p (j c) -> p j c", j=QT)
        hid = area0[:, 0:2 * FGRP * HALF].rearrange("p (s f t) -> p s f t", s=2, f=FGRP)

        pB = ctx.enter_context(nc.psum_tensor("pB", [128, L], F32))
        pC = ctx.enter_context(nc.psum_tensor("pC", [128, L], F32))
        pW = ctx.enter_context(nc.psum_tensor("pW", [128, 4, HALF], F32))
        pS = pW[:, 0:2, :].rearrange("p b t -> p (b t)")

        consts_in, prep_act, prep_dve, prep_pe, prep_pool = (
            sem(n) for n in ("consts_in", "prep_act", "prep_dve", "prep_pe", "prep_pool"))
        x_in, win_in, out_dma = (sem(n) for n in ("x_in", "win_in", "out_dma"))
        pad_zero, sq_ready, ms_ready, ms_log, rstd_ready, xn_ready, ip_ready, ip_evac = (
            sem(n) for n in ("pad_zero", "sq_ready", "ms_ready", "ms_log", "rstd_ready", "xn_ready", "ip_ready",
                             "ip_evac"))
        dw_step, sig_ready, loc_ready, xres_ready, cv_step, uc_ready = (
            sem(n) for n in ("dw_step", "sig_ready", "loc_ready", "xres_ready", "cv_step", "uc_ready"))
        xd_ready, xd_evac, split_step, yd_ready = (sem(n) for n in ("xd_ready", "xd_evac", "split_step", "yd_ready"))
        dt_ready, relu_done, sp_abs, sp_exp, sp_ready, delta_ready, du_ready = (
            sem(n) for n in ("dt_ready", "relu_done", "sp_abs", "sp_exp", "sp_ready", "delta_ready", "du_ready"))
        b_ready, c_ready, da_ready, m1_done, scan_done, m2_done, y_done = (
            sem(n) for n in ("b_ready", "c_ready", "da_ready", "m1_done", "scan_done", "m2_done", "y_done"))
        yz_ready, op_ready, xa_ready = (sem(n) for n in ("yz_ready", "op_ready", "xa_ready"))
        ln_mean, ln_xc, ln_sq, ln_var, ln_log, ln_rs, ln_xn = (
            sem(n) for n in ("ln_mean", "ln_xc", "ln_sq", "ln_var", "ln_log", "ln_rs", "ln_xn"))
        pj_ready, pj_evac, s_ready, nmax_ready, p_ready, tr_ready, pt_ready, pv_done, rinv_ready, ctx_ready = (
            sem(n) for n in ("pj_ready", "pj_evac", "s_ready", "nmax_ready", "p_ready", "tr_ready", "pt_ready",
                             "pv_done", "rinv_ready", "ctx_ready"))
        ct_ready, ct_evac, wo_ready, wo_add = (sem(n) for n in ("ct_ready", "ct_evac", "wo_ready", "wo_add"))
        xr_ready, xr_evac, fc_ready, h_ready, r_done, r_evac, fo_ready, x2_ready = (
            sem(n) for n in ("xr_ready", "xr_evac", "fc_ready", "h_ready", "r_done", "r_evac", "fo_ready",
                             "x2_ready"))

        def at(per, b, n):
            v = b * per + n
            return max(v, 0) if isinstance(v, int) else v

        def samples(eng, iteration):
            iteration(0, True, False)
            with eng.Fori(1, NB) as b:
                iteration(b, True, True)
            iteration(NB, False, True)

        def rows(d):
            return [(d * DROWS + n * KT + k, n, k) for n in range(NS) for k in range(KT)]

        def flow(d, ap):
            return ap if d == 0 else ap[:, ::-1]

        block = ctx.enter_context(nc.Block())

        @block.sync
        def _(sp):
            def load_x(b):
                sp.wait_ge(xa_ready, at(6, b, 0))
                sp.dma_start(xres[:, :, :], x[b].rearrange("(k p) t -> p k t", p=128)).then_inc(x_in, 16)

            sp.dma_start(ip_w, w_in.rearrange("(k p) e -> p k e", p=128)).then_inc(win_in, 16)
            load_x(0)
            for dst, src in ((vec[:, :, :], chan.rearrange("(k p) v -> p k v", p=128)),
                             (consts[:, :], k128[:, :]),
                             (small[0:1, 0:2], scal[:, :]),
                             (prob[0:KI, 0:2 * C], k32[:, :]),
                             (small[0:12, 2:3], fc2[:, :]),
                             (small[0:12, 3:4], pr2[:, :]),
                             (xp_w[:, :, :], w_x.rearrange("(k p) e -> p k e", p=128)),
                             (dt_w[0], w_dt[:, :]), (dt_w[1], w_dt[:, :]),
                             (op_w[:, :, :], w_out.rearrange("(k p) e -> p k e", p=128)),
                             (q_w[:, :, :], wq.rearrange("(k p) e -> p k e", p=128)),
                             (k_w[:, :, :], wk.rearrange("(k p) e -> p k e", p=128)),
                             (v_w[:, :, :], wv.rearrange("(k p) e -> p k e", p=128)),
                             (o_w[:, :, :], wo.rearrange("(k p) e -> p k e", p=128)),
                             (fc_w, fc1[:, :]),
                             (pr_w[:, :, :], pr1.rearrange("(f p) i -> p f i", p=128))):
                sp.dma_start(dst, src).then_inc(consts_in, 16)

            def iteration(b, layer0, layer1):
                if layer0 and not (isinstance(b, int) and b == 0):
                    load_x(b)
                if layer1:
                    if layer0:
                        sp.wait_ge(ct_evac, at(6, b, 0))
                        sp.dma_start(ip_w, w_in.rearrange("(k p) e -> p k e", p=128)).then_inc(win_in, 16)
                    sp.wait_ge(x2_ready, at(2, b, 0))
                    a = b - 1
                    sp.dma_start(out[a].rearrange("(k p) t -> p k t", p=128), xa[:, :, :]).then_inc(out_dma, 16)

            samples(sp, iteration)
            sp.wait_ge(out_dma, 16 * NB)
            sp.wait_ge(win_in, 16 * NB)

        NCONST = 16 * 16

        @block.tensor
        def _(pe):
            pe.wait_ge(consts_in, NCONST)
            rep = prob[0:12, C:2 * C]
            for k in range(KT):
                pe.matmul(pW[:, 0, k:k + 1], rep[:, 128 * k:128 * k + 128], small[0:12, 2:3], start=True, stop=True)
            pe.matmul(pW[0:KI, 1, 0:C], small[0:12, 3:4].broadcast_to([12, KI]), rep, start=True, stop=True)
            pe.wait_ge(prep_pool, 1)
            pe.matmul(pW[:, 2, 0:2], small[0:1, 32:33].broadcast_to([1, 128]), small[0:1, 0:2],
                      start=True, stop=True).then_inc(prep_pe, 1)
            pe.wait_ge(prep_dve, 1)

            def project(bank, w, cols, src, toks, done):
                for k in range(KT):
                    mm = pe.matmul(bank, w[:, k, cols], src[:, k, toks], start=(k == 0), stop=(k == KT - 1))
                mm.then_inc(done, 1)

            def average(bank, src, toks, done):
                for k in range(KT):
                    mm = pe.matmul(bank, ones_c, src[:, k, toks], start=(k == 0), stop=(k == KT - 1))
                mm.then_inc(done, 1)

            def step_sizes(b, d):
                for k in range(KT):
                    bank = (pB, pC)[k % 2]
                    if k == 0:
                        pe.wait_ge(xd_evac, at(4, b, 2 + 2 * d))
                        pe.wait_ge(m2_done, at(ROWS, b, DROWS * d))
                        pe.wait_ge(y_done, at(ROWS, b, DROWS * d - 3))
                    if k == 2:
                        pe.wait_ge(relu_done, at(6, b, 3 * d + 1))
                        pe.wait_ge(sp_abs, at(6, b, 3 * d + 1))
                    for c in range(2):
                        mm = pe.matmul(bank[:, c * HALF:(c + 1) * HALF], dt_w[d][:, 128 * k:128 * k + 128],
                                       dtr[d][:, c * HALF:(c + 1) * HALF], start=True, stop=True)
                    mm.then_inc(dt_ready, 1)

            def spread(b, d, n, bank, row, done):
                for c in range(2):
                    mm = pe.matmul(bank[:, c * HALF:(c + 1) * HALF], sel_bf[0:96, row:row + 1].broadcast_to([96, 128]),
                                   bc3[d][:, c * HALF:(c + 1) * HALF], start=True, stop=True)
                mm.then_inc(done, 1)

            def spread_b(b, d, n):
                if n == 0:
                    pe.wait_ge(split_step, at(10, b, 5 * (d + 1)))
                    pe.wait_ge(delta_ready, at(6, b, 3 * (d + 1)))
                else:
                    pe.wait_ge(m1_done, at(ROWS, b, DROWS * d + KT * n))
                spread(b, d, n, pB, n, b_ready)

            def spread_c(b, d, n):
                if n:
                    pe.wait_ge(m2_done, at(ROWS, b, DROWS * d + KT * n))
                spread(b, d, n, pC, NS + n, c_ready)

            def item(kind, n, b):
                a = b - 1
                if kind == "ln_mean":
                    for c in range(2):
                        if n == 0:
                            pe.wait_ge(xa_ready, at(6, a, 6))
                            if isinstance(b, int):
                                pe.wait_ge(xd_evac, at(4, NB, 0))
                            else:
                                pe.wait_ge(xd_evac, at(4, b, 4))
                        else:
                            pe.wait_ge(wo_add, at(6, a, 6))
                        average(pW[:, 2 * c, :], xa, slice(c * HALF, (c + 1) * HALF), ln_mean)
                elif kind == "ln_var":
                    for c in range(2):
                        pe.wait_ge(ln_sq, at(4, a, 2 * n + c + 1))
                        average(pW[:, 2 * c + 1, :], sq_of[n],
                                slice(c * HALF, (c + 1) * HALF), ln_var)
                elif kind == "proj":
                    pe.wait_ge(ln_xn, at(4, a, 2))
                    if n >= 4:
                        pe.wait_ge(pj_evac, at(NPJ, a, n - 3))
                    bank = pW[:, n % 4, :]
                    if n < 12:
                        m, c = n % 6 // 2, n % 2
                        project(bank, (q_w, k_w)[n // 6], slice(128 * m, 128 * m + 128), xn1,
                                slice(c * HALF, (c + 1) * HALF), pj_ready)
                    else:
                        j = n - 12
                        for k in range(KT):
                            mm = pe.matmul(bank[:, 0:C], xn1[:, k, 128 * j:128 * j + 128], v_w[:, k, :],
                                           start=(k == 0), stop=(k == KT - 1))
                        mm.then_inc(pj_ready, 1)
                elif kind == "attend":
                    def turn(g):
                        s, k0, nk = GROUPS[g]
                        pe.wait_ge(p_ready, at(NT, a, s + 1))
                        if g:
                            pe.wait_ge(pt_ready, at(NG, a, g))
                        for j in range(nk):
                            mm = pe.transpose(pW[:, 2, 128 * j:128 * j + 128],
                                              prob[:, 128 * (k0 + j):128 * (k0 + j) + 128], ident)
                        mm.then_inc(tr_ready, 1)

                    def values(g):
                        s, k0, nk = GROUPS[g]
                        h, i = TILES[s]
                        pe.wait_ge(pt_ready, at(NG, a, g + 1))
                        if k0 == 0 and s:
                            pe.wait_ge(ctx_ready, at(NT, a, s))
                        for j in range(nk):
                            mm = pe.matmul(pW[:, 3, 0:DH], pt[:, g % 2, 128 * j:128 * j + 128],
                                           vtok[:, k0 + j, DH * h:DH * h + DH],
                                           start=(k0 + j == 0), stop=(k0 + j == i))
                        mm.then_inc(pv_done, 1)

                    if n >= 2:
                        values(FIRST_GROUP[n - 1] - 1)
                    if 1 <= n <= NT:
                        turn(FIRST_GROUP[n - 1])
                    if n < NT:
                        h, i = TILES[n]
                        p0 = DH * (h % 2)
                        pe.wait_ge(pj_evac, at(NPJ, a, NPJ))
                        if n:
                            pe.wait_ge(p_ready, at(NT, a, n))
                        keys = 128 * (i + 1)
                        for c0 in range(0, keys, HALF):
                            w = min(HALF, keys - c0)
                            own = c0 + w == keys
                            mm = pe.matmul(pS[:, c0:c0 + w], qT[p0:p0 + DH, h // 2, 128 * i:128 * i + 128],
                                           kT[p0:p0 + DH, h // 2, c0:c0 + w], start=True, stop=not own)
                        mm = pe.matmul(pS[:, keys - 128:keys], ident_bf[:, :], causal_bf[:, :], start=False, stop=True)
                        mm.then_inc(s_ready, 1)
                    if 1 <= n <= NT and FIRST_GROUP[n] - FIRST_GROUP[n - 1] == 2:
                        turn(FIRST_GROUP[n - 1] + 1)
                        values(FIRST_GROUP[n - 1])
                elif kind == "ctx_t":
                    m, c = n // 2, n % 2
                    pe.wait_ge(ctx_ready, at(NT, a, NT))
                    if n >= 4:
                        pe.wait_ge(ct_evac, at(6, a, n - 3))
                    for j in range(4):
                        mm = pe.transpose(pW[:, n % 4, 128 * j:128 * j + 128],
                                          ctxk[:, 4 * c + j, 128 * m:128 * m + 128], ident)
                    mm.then_inc(ct_ready, 1)
                elif kind == "wo":
                    m, c = n // 2, n % 2
                    pe.wait_ge(ct_evac, at(6, a, 6))
                    if n >= 4:
                        pe.wait_ge(wo_add, at(6, a, n - 3))
                    project(pW[:, n % 4, :], o_w, slice(128 * m, 128 * m + 128), ctxT,
                            slice(c * HALF, (c + 1) * HALF), wo_ready)
                elif kind == "mlp_in":
                    pe.wait_ge(ln_xn, at(4, a, 4))
                    for c in range(2):
                        project(pW[0:KI, c, :], kin_w, slice(0, KI), xn2, slice(c * HALF, (c + 1) * HALF), xr_ready)
                elif kind == "mlp":
                    c, q = n // (NFG + 1), n % (NFG + 1)
                    g = c * NFG + q
                    toks = slice(c * HALF, (c + 1) * HALF)

                    def hidden():
                        pe.wait_ge(xr_evac, at(2, a, 2))
                        if g:
                            pe.wait_ge(h_ready, at(2 * NFG, a, g))
                        if q == 0 and c:
                            pe.wait_ge(x2_ready, at(2, a, c))
                        for f in range(FGRP):
                            ft = FGRP * q + f
                            mm = pe.matmul(pW[:, f, :], fc_w[:, 128 * ft:128 * ft + 128], xr[:, toks],
                                           start=True, stop=True)
                        mm.then_inc(fc_ready, 1)

                    if q < NFG:
                        hidden()
                    if q >= 1:
                        pe.wait_ge(h_ready, at(2 * NFG, a, g))
                        if q == 1 and c:
                            pe.wait_ge(r_evac, at(2, a, c))
                        for f in range(FGRP):
                            ft = FGRP * (q - 1) + f
                            mm = pe.matmul(pW[0:KI, 3, :], pr_w[:, ft, :], hid[:, (g - 1) % 2, f, :],
                                           start=(ft == 0), stop=(ft == NF - 1))
                        mm.then_inc(r_done, 1)
                elif kind == "mlp_out":
                    pe.wait_ge(r_evac, at(2, a, n + 1))
                    for m in range(KT):
                        mm = pe.matmul(pW[:, m, :], kout_w[:, 128 * m:128 * m + 128],
                                       rr[:, n * HALF:(n + 1) * HALF], start=True, stop=True)
                    mm.then_inc(fo_ready, 1)

            def iteration(b, layer0, layer1):
                if layer0:
                    pe.wait_ge(m2_done, at(ROWS, b, 0))
                    pe.wait_ge(sq_ready, at(3, b, 3))
                    for c in range(2):
                        average(pB[:, c * HALF:(c + 1) * HALF], uc_f,
                                slice(c * HALF, (c + 1) * HALF), ms_ready)
                    pe.wait_ge(xn_ready, at(3, b, 3))
                    if isinstance(b, int):
                        pe.wait_ge(win_in, 16)
                    else:
                        pe.wait_ge(win_in, at(16, b, 0))
                    pe.wait_ge(xa_ready, at(6, b, 0))
                    for t in range(12):
                        m, c = t // 2, t % 2
                        if t >= 4:
                            pe.wait_ge(ip_evac, at(12, b, t - 3))
                        for k in range(KT):
                            mm = pe.matmul(pW[:, t % 4, :], ip_w[:, k, 128 * m:128 * m + 128],
                                           xnp[:, k, 1 + 16 * c:17 + 16 * c, 1:1 + WW],
                                           start=(k == 0), stop=(k == KT - 1))
                        mm.then_inc(ip_ready, 1)
                    pe.wait_ge(ip_evac, at(12, b, 12))
                    for d in range(2):
                        pe.wait_ge(uc_ready, at(6, b, 3 * d + 3))
                        for c in range(2):
                            for k in range(KT):
                                mm = pe.matmul(pW[0:56, 2 * d + c, :], xp_w[:, k, :],
                                               uc[d][:, k, c * HALF:(c + 1) * HALF], start=(k == 0), stop=(k == KT - 1))
                        mm.then_inc(xd_ready, 1)
                if layer0:
                    for d in range(2):
                        step_sizes(b, d)
                        spread_b(b, d, 0)
                        for r, n, k in rows(d):
                            if layer1:
                                for kind, i in SLOTS[r]:
                                    item(kind, i, b)
                            if k == 2 and n + 1 < NS:
                                spread_b(b, d, n + 1)
                            if k == 0:
                                spread_c(b, d, n)
                    for t in range(6):
                        m, c = t // 2, t % 2
                        if t == 0:
                            pe.wait_ge(yz_ready, at(3, b, 3))
                            pe.wait_ge(x2_ready, at(2, b, 0))
                        if t >= 4:
                            pe.wait_ge(xa_ready, at(6, b, t - 3))
                        project(pW[:, t % 4, :], op_w, slice(128 * m, 128 * m + 128), y,
                                slice(c * HALF, (c + 1) * HALF), op_ready)
                else:
                    for kind, i, _ in ITEMS:
                        item(kind, i, b)

            samples(pe, iteration)

        @block.scalar
        def _(act):
            act.wait_ge(consts_in, NCONST)
            act.wait_ge(prep_pool, 3)
            act.activation(vec[:, :, V_A:V_A + NS], vec[:, :, V_A:V_A + NS], ACT.Exp).then_inc(prep_act, 1)
            act.copy(ident_bf[:, :], consts[:, 0:128])
            act.copy(causal_bf[:, :], consts[:, 128:256])
            act.copy(sel_bf[:, :], consts[:, 384:416]).then_inc(prep_act, 1)
            act.wait_ge(prep_dve, 1)

            def step_sizes(b, d):
                for k in range(KT):
                    t = dA[k % 2]
                    if k < 2:
                        act.wait_ge(scan_done, at(ROWS, b, DROWS * d))
                        act.wait_ge(xn_ready, at(3, b, 3))
                    else:
                        act.wait_ge(delta_ready, at(6, b, 3 * d + 1))
                    act.wait_ge(dt_ready, at(6, b, 3 * d + k + 1))
                    act.activation(t[:, :], (pB, pC)[k % 2][:, :], ACT.Abs,
                                   bias=vec[:, k, V_DTB:V_DTB + 1]).then_inc(sp_abs, 1)
                    act.wait_ge(sp_abs, at(6, b, 3 * d + k + 1))
                    act.activation(t[:, :], t[:, :], ACT.Exp, scale=-1.0).then_inc(sp_exp, 1)
                    act.wait_ge(sp_exp, at(6, b, 3 * d + k + 1))
                    act.activation(t[:, :], t[:, :], ACT.Ln, bias=1.0).then_inc(sp_ready, 1)

            def decay(b, r):
                d, k = r // DROWS, r % KT
                n = r % DROWS // KT
                act.wait_ge(scan_done, at(ROWS, b, r - 1))
                if r % DROWS < KT:
                    act.wait_ge(delta_ready, at(6, b, 3 * d + 3))
                act.activation(dA[r % 2][:, :], delta[:, k, :], ACT.Exp,
                               scale=vec[:, k, V_A + n:V_A + n + 1]).then_inc(da_ready, 1)

            def item(kind, n, b, early):
                a = b - 1
                if kind == "ln_var" and early:
                    for c in range(2):
                        if n == 0:
                            if isinstance(b, int):
                                act.wait_ge(du_ready, at(6, NB, 0))
                            else:
                                act.wait_ge(du_ready, at(6, b, 3))
                        act.wait_ge(ln_xc, at(4, a, 2 * n + c + 1))
                        toks = slice(c * HALF, (c + 1) * HALF)
                        act.activation(sq_of[n][:, :, toks], lnx_of[n][:, :, toks], ACT.Square).then_inc(ln_sq, 1)
                elif kind == "ln_scale" and early:
                    for c in range(2):
                        act.wait_ge(ln_var, at(4, a, 2 * n + c + 1))
                        act.activation(prob[:, c * HALF:(c + 1) * HALF], pW[:, 2 * c + 1, :], ACT.Ln,
                                       bias=eps5).then_inc(ln_log, 1)
                    for c in range(2):
                        act.wait_ge(ln_log, at(4, a, 2 * n + c + 1))
                        act.activation(prob[:, c * HALF:(c + 1) * HALF], prob[:, c * HALF:(c + 1) * HALF], ACT.Exp,
                                       scale=-0.5).then_inc(ln_rs, 1)
                elif kind == "proj" and not early:
                    act.wait_ge(pj_ready, at(NPJ, a, n + 1))
                    act.wait_ge(ln_var, at(4, a, 2))
                    bank = pW[:, n % 4, :]
                    if n < 12:
                        m, c = n % 6 // 2, n % 2
                        toks = slice(c * HALF, (c + 1) * HALF)
                        if n < 6:
                            ev = act.activation(qT[:, m, toks], bank, ACT.Identity, bias=bq_s[:, m:m + 1], scale=0.125)
                        else:
                            ev = act.activation(kT[:, m, toks], bank, ACT.Identity, bias=vec[:, m, V_BK:V_BK + 1])
                    else:
                        ev = act.copy(vtok[:, n - 12, :], bank[:, 0:C])
                    ev.then_inc(pj_evac, 1)
                elif kind == "attend":
                    def spill(g):
                        s, k0, nk = GROUPS[g]
                        act.wait_ge(tr_ready, at(NG, a, g + 1))
                        if g >= 2:
                            act.wait_ge(pv_done, at(NG, a, g - 1))
                        act.copy(pt[:, g % 2, 0:128 * nk], pW[:, 2, 0:128 * nk]).then_inc(pt_ready, 1)

                    if not 1 <= n <= NT:
                        return
                    s = n - 1
                    keys = 128 * (TILES[s][1] + 1)
                    if early:
                        act.wait_ge(nmax_ready, at(NT, a, s + 1))
                        if s:
                            act.wait_ge(tr_ready, at(NG, a, FIRST_GROUP[s]))
                        else:
                            act.wait_ge(ln_xn, at(4, a, 2))
                        if s >= 2:
                            act.wait_ge(ctx_ready, at(NT, a, s - 1))
                        act.activation(prob[:, 0:keys], pS[:, 0:keys], ACT.Exp, bias=stat[:, 0, s % 2:s % 2 + 1],
                                       accum_out=stat[:, 1, s % 2:s % 2 + 1]).then_inc(p_ready, 1)
                    else:
                        for g in range(FIRST_GROUP[s], FIRST_GROUP[s + 1]):
                            spill(g)
                elif kind == "ctx_t" and not early:
                    m, c = n // 2, n % 2
                    act.wait_ge(ct_ready, at(6, a, n + 1))
                    act.activation(ctxT[:, m, c * HALF:(c + 1) * HALF], pW[:, n % 4, :], ACT.Identity,
                                   bias=vec[:, m, V_BV:V_BV + 1]).then_inc(ct_evac, 1)
                elif kind == "mlp_in" and not early:
                    for c in range(2):
                        act.wait_ge(xr_ready, at(2, a, c + 1))
                        act.copy(xr[:, c * HALF:(c + 1) * HALF], pW[0:KI, c, :]).then_inc(xr_evac, 1)
                elif kind == "mlp" and not early:
                    c, q = n // (NFG + 1), n % (NFG + 1)
                    g = c * NFG + q
                    if q < NFG:
                        act.wait_ge(fc_ready, at(2 * NFG, a, g + 1))
                        if g >= 2:
                            act.wait_ge(r_done, at(2 * NFG, a, g - 1))
                        act.activation(hid[:, g % 2, :, :], pW[:, 0:FGRP, :], ACT.Gelu).then_inc(h_ready, 1)
                    else:
                        act.wait_ge(r_done, at(2 * NFG, a, g))
                        act.copy(rr[:, c * HALF:(c + 1) * HALF], pW[0:KI, 3, :]).then_inc(r_evac, 1)

            def iteration(b, layer0, layer1):
                if layer0:
                    act.wait_ge(xa_ready, at(6, b, 0))
                    for k in range(KT):
                        act.wait_ge(x_in, at(16, b, 16))
                        act.activation(uc_f[:, k, :], xres[:, k, :], ACT.Square).then_inc(sq_ready, 1)
                    act.wait_ge(ms_ready, at(2, b, 2))
                    act.wait_ge(scan_done, at(ROWS, b, 0))
                    act.activation(dA[0][:, :], pB[:, :], ACT.Ln, bias=eps6).then_inc(ms_log, 1)
                    act.wait_ge(ms_log, at(1, b, 1))
                    act.activation(dA[0][:, :], dA[0][:, :], ACT.Exp, scale=-0.5).then_inc(rstd_ready, 1)
                    for t in range(6):
                        m, c = t // 2, t % 2
                        act.wait_ge(ip_ready, at(12, b, t + 1))
                        act.wait_ge(pad_zero, at(6, b, 6))
                        act.copy(up[:, m, NTAP - 1 + c * HALF:NTAP - 1 + (c + 1) * HALF],
                                 pW[:, t % 4, :]).then_inc(ip_evac, 1)
                    for t in range(6, 12):
                        m, c = t // 2 - 3, t % 2
                        act.wait_ge(ip_ready, at(12, b, t + 1))
                        act.wait_ge(yz_ready, at(3, b, 0))
                        act.activation(zs[:, m, c * HALF:(c + 1) * HALF], pW[:, t % 4, :], ACT.Silu).then_inc(ip_evac, 1)
                    for k in range(KT):
                        act.wait_ge(dw_step, at(27, b, 24 + k + 1))
                        act.activation(y[:, k, :], y[:, k, :], ACT.Sigmoid).then_inc(sig_ready, 1)
                    for d in range(2):
                        for k in range(KT):
                            act.wait_ge(cv_step, at(24, b, 12 * d + 9 + k + 1))
                            act.activation(uc[d][:, k, :], uc[d][:, k, :], ACT.Silu,
                                           bias=vec[:, k, V_CB:V_CB + 1]).then_inc(uc_ready, 1)
                    for d in range(2):
                        act.wait_ge(xd_ready, at(2, b, d + 1))
                        act.wait_ge(y_done, at(ROWS, b, 0))
                        act.copy(hb[d][0:32, :], pW[0:32, 2 * d:2 * d + 2, :].rearrange("p b t -> p (b t)"))\
                            .then_inc(xd_evac, 1)
                        act.copy(dtr[d], pW[32:56, 2 * d:2 * d + 2, :].rearrange("p b t -> p (b t)"))\
                            .then_inc(xd_evac, 1)
                    for d in range(2):
                        step_sizes(b, d)
                        decay(b, DROWS * d)
                        for r, n, k in rows(d):
                            for kind, i in SLOTS[r] if layer1 else ():
                                item(kind, i, b, True)
                            if r + 1 < DROWS * (d + 1):
                                decay(b, r + 1)
                            for kind, i in SLOTS[r] if layer1 else ():
                                item(kind, i, b, False)
                else:
                    for kind, i, _ in ITEMS:
                        item(kind, i, b, True)
                        item(kind, i, b, False)

            samples(act, iteration)

        @block.vector
        def _(dve):
            dve.memset(eps6, 1e-6)
            dve.memset(eps5, 1e-5)
            dve.wait_ge(prep_act, 2)
            dve.tensor_scalar(vec[:, :, V_A:V_A + NS], vec[:, :, V_A:V_A + NS], -1.0, None, ALU.mult)
            dve.tensor_scalar(bq_s, vec[:, :, V_BQ], 0.125, None, ALU.mult)
            dve.wait_ge(prep_pe, 1)
            for k in range(KT):
                dve.tensor_scalar(kin_w[:, k, :], consts[:, 416 + KI * k:448 + KI * k] if k < 3 else None,
                                  pW[:, 0, k:k + 1], None, ALU.mult)
            dve.tensor_tensor(kout_w, prob[0:KI, 0:C], pW[0:KI, 1, 0:C], ALU.mult)
            dve.tensor_copy(small[:, 8:10], pW[:, 2, 0:2]).then_inc(prep_dve, 0 + 1)
            dve.wait_ge(prep_dve, 1)
            dve.tensor_copy(rs_col, small[:, 9:10])
            dve.tensor_tensor(g_col, small[:, 8:9], small[:, 9:10], ALU.mult).then_inc(prep_dve, 1)
            dve.wait_ge(prep_dve, 2)

            def step_sizes(b, d):
                for k in range(KT):
                    dve.wait_ge(sp_abs, at(6, b, 3 * d + k + 1))
                    dve.wait_ge(da_ready, at(ROWS, b, DROWS * d))
                    dve.tensor_scalar(delta[:, k, :], (pB, pC)[k % 2][:, :], vec[:, k, V_DTB:V_DTB + 1], 0.0,
                                      ALU.add, ALU.max).then_inc(relu_done, 1)
                    dve.wait_ge(relu_done, at(6, b, 3 * d + k + 1))
                    dve.wait_ge(sp_ready, at(6, b, 3 * d + k + 1))
                    dve.tensor_tensor(delta[:, k, :], delta[:, k, :], dA[k % 2][:, :], ALU.add)\
                       .then_inc(delta_ready, 1)
                for k in range(KT):
                    dve.wait_ge(delta_ready, at(6, b, 3 * d + k + 1))
                    dve.wait_ge(m1_done, at(ROWS, b, DROWS * d))
                    dve.tensor_tensor(du[d][:, k, :], delta[:, k, :], uc[d][:, k, :], ALU.mult)\
                       .then_inc(du_ready, 1)

            def input_row(b, r, n, k, d):
                if k == 0:
                    dve.wait_ge(b_ready, at(2 * NS, b, NS * d + n + 1))
                dve.wait_ge(y_done, at(ROWS, b, r - 2))
                if n == 0:
                    dve.wait_ge(du_ready, at(6, b, 3 * d + k + 1))
                    dve.wait_ge(split_step, at(10, b, 10))
                dve.tensor_tensor(hb[r % 3][:, :], du[d][:, k, :], pB[:, :], ALU.mult).then_inc(m1_done, 1)

            def scan_row(b, r, d):
                dve.wait_ge(da_ready, at(ROWS, b, r + 1))
                dve.wait_ge(m1_done, at(ROWS, b, r + 1))
                buf = hb[r % 3]
                dve.tensor_tensor_scan(flow(d, buf[:, :]), flow(d, dA[r % 2][:, :]), flow(d, buf[:, :]), 0.0,
                                       ALU.mult, ALU.add).then_inc(scan_done, 1)

            def output_row(b, r, n, k, d):
                if k == 0:
                    dve.wait_ge(c_ready, at(2 * NS, b, NS * d + n + 1))
                dve.wait_ge(scan_done, at(ROWS, b, r + 1))
                dve.tensor_tensor(hb[r % 3][:, :], hb[r % 3][:, :], pC[:, :], ALU.mult).then_inc(m2_done, 1)

            def item(kind, n, b, early):
                a = b - 1
                if kind == "ln_mean" and not early:
                    for c in range(2):
                        toks = slice(c * HALF, (c + 1) * HALF)
                        if n == 0:
                            if isinstance(b, int):
                                dve.wait_ge(ip_ready, at(12, NB, 0))
                            else:
                                dve.wait_ge(ip_ready, at(12, b, 12))
                        dve.wait_ge(ln_mean, at(4, a, 2 * n + c + 1))
                        dve.tensor_tensor(lnx_of[n][:, :, toks], xa[:, :, toks],
                                          pW[:, 2 * c:2 * c + 1, :].broadcast_to([128, KT, HALF]),
                                          ALU.subtract).then_inc(ln_xc, 1)
                elif kind == "attend":
                    if early and 1 <= n <= NT:
                        s = n - 1
                        keys = 128 * (TILES[s][1] + 1)
                        dve.wait_ge(s_ready, at(NT, a, s + 1))
                        if s >= 2:
                            dve.wait_ge(p_ready, at(NT, a, s - 1))
                        dve.tensor_reduce(stat[:, 0, s % 2:s % 2 + 1], pS[:, 0:keys], AX, ALU.max, negate=True)\
                           .then_inc(nmax_ready, 1)
                    if not early and n >= 2:
                        s = n - 2
                        h, i = TILES[s]
                        dve.wait_ge(p_ready, at(NT, a, s + 1))
                        dve.reciprocal(stat[:, 2, s % 2:s % 2 + 1], stat[:, 1, s % 2:s % 2 + 1]).then_inc(rinv_ready, 1)
                        dve.wait_ge(rinv_ready, at(NT, a, s + 1))
                        dve.wait_ge(pv_done, at(NG, a, FIRST_GROUP[s + 1]))
                        dve.tensor_scalar(ctxk[:, i, DH * h:DH * h + DH], pW[:, 3, 0:DH],
                                          stat[:, 2, s % 2:s % 2 + 1], None, ALU.mult).then_inc(ctx_ready, 1)
                elif kind == "wo" and not early:
                    m, c = n // 2, n % 2
                    toks = slice(c * HALF, (c + 1) * HALF)
                    dve.wait_ge(wo_ready, at(6, a, n + 1))
                    dve.scalar_tensor_tensor(out=xa[:, m, toks], in0=pW[:, n % 4, :], scalar=vec[:, m, V_BO:V_BO + 1],
                                             in1=xa[:, m, toks], op0=ALU.add, op1=ALU.add).then_inc(wo_add, 1)
                elif kind == "mlp_out" and not early:
                    toks = slice(n * HALF, (n + 1) * HALF)
                    dve.wait_ge(fo_ready, at(2, a, n + 1))
                    dve.wait_ge(wo_add, at(6, a, 6))
                    dve.tensor_tensor(xa[:, :, toks], xa[:, :, toks], pW[:, 0:3, :], ALU.add).then_inc(x2_ready, 1)

            def iteration(b, layer0, layer1):
                if layer0:
                    dve.wait_ge(xa_ready, at(6, b, 0))
                    for border in (xnp[:, :, 0, :], xnp[:, :, HH + 1, :], xnp[:, :, 1:1 + HH, 0:1],
                                   xnp[:, :, 1:1 + HH, WW + 1:WP], up[:, :, 0:NTAP - 1], up[:, :, UP - NTAP + 1:UP]):
                        dve.memset(border, 0.0).then_inc(pad_zero, 1)
                    dve.wait_ge(x_in, at(16, b, 16))
                    dve.wait_ge(pad_zero, at(6, b, 6))
                    for k in range(KT):
                        dve.wait_ge(rstd_ready, at(1, b, 1))
                        dve.scalar_tensor_tensor(out=xnp[:, k, 1:1 + HH, 1:1 + WW],
                                                 in0=xres[:, k, :].rearrange("p (h w) -> p h w", w=WW),
                                                 scalar=vec[:, k, V_NW:V_NW + 1],
                                                 in1=dA[0][:, :].rearrange("p (h w) -> p h w", w=WW),
                                                 op0=ALU.mult, op1=ALU.mult).then_inc(xn_ready, 1)
                    dve.wait_ge(op_ready, at(6, b, 0))
                    for j in range(9):
                        for k in range(KT):
                            step = KT * j + k
                            win = xnp[:, k, j // 3:j // 3 + HH, j % 3:j % 3 + WW]
                            acc = y[:, k, :].rearrange("p (h w) -> p h w", w=WW)
                            w = vec[:, k, V_DW + j:V_DW + j + 1]
                            if j == 0:
                                dve.wait_ge(xn_ready, at(3, b, k + 1))
                                dve.tensor_scalar(acc, win, w, vec[:, k, V_DWB:V_DWB + 1], ALU.mult, ALU.add)\
                                   .then_inc(dw_step, 1)
                            else:
                                dve.wait_ge(dw_step, at(27, b, step - 2))
                                dve.scalar_tensor_tensor(out=acc, in0=win, scalar=w, in1=acc, op0=ALU.mult,
                                                         op1=ALU.add).then_inc(dw_step, 1)
                    for d in range(2):
                        for j in range(NTAP):
                            for k in range(KT):
                                step = 12 * d + KT * j + k
                                off = j if d == 0 else 2 * (NTAP - 1) - j
                                src, w = up[:, k, off:off + L], vec[:, k, V_CW + j:V_CW + j + 1]
                                if j == 0:
                                    dve.wait_ge(ip_evac, at(12, b, 2 * k + 2))
                                    dve.wait_ge(ms_ready, at(2, b, 2))
                                    dve.wait_ge(m1_done, at(ROWS, b, 0))
                                    dve.tensor_scalar(uc[d][:, k, :], src, w, None, ALU.mult).then_inc(cv_step, 1)
                                else:
                                    dve.wait_ge(cv_step, at(24, b, step - 2))
                                    dve.scalar_tensor_tensor(out=uc[d][:, k, :], in0=src, scalar=w,
                                                             in1=uc[d][:, k, :], op0=ALU.mult, op1=ALU.add)\
                                       .then_inc(cv_step, 1)
                    for k in range(KT):
                        dve.wait_ge(sig_ready, at(3, b, k + 1))
                        acc = y[:, k, :].rearrange("p (h w) -> p h w", w=WW)
                        dve.scalar_tensor_tensor(out=acc, in0=acc, scalar=rs_col, in1=xnp[:, k, 1:1 + HH, 1:1 + WW],
                                                 op0=ALU.mult, op1=ALU.mult).then_inc(loc_ready, 1)
                    low = hb[2][0:32, 0:HALF].bitcast(BF16)
                    for d in range(2):
                        rest, parts = hb[d][0:32, :], bc3[d]
                        dve.wait_ge(xd_evac, at(4, b, 2 * d + 1))
                        dve.wait_ge(c_ready, at(2 * NS, b, 0))
                        dve.tensor_copy(parts[0:32, :], rest).then_inc(split_step, 1)
                        dve.wait_ge(split_step, at(10, b, 5 * d + 1))
                        dve.tensor_tensor(rest, rest, parts[0:32, :], ALU.subtract).then_inc(split_step, 1)
                        dve.wait_ge(split_step, at(10, b, 5 * d + 2))
                        dve.tensor_copy(low, rest).then_inc(split_step, 1)
                        dve.wait_ge(split_step, at(10, b, 5 * d + 3))
                        dve.tensor_tensor(parts[64:96, :], rest, low, ALU.subtract).then_inc(split_step, 1)
                        dve.tensor_copy(parts[32:64, :], low).then_inc(split_step, 1)
                    for d in range(2):
                        for k in range(KT):
                            dve.wait_ge(uc_ready, at(6, b, 3 * d + k + 1))
                            dcol = vec[:, k, V_D:V_D + 1]
                            if d == 0:
                                dve.wait_ge(xres_ready, at(3, b, k + 1))
                                dve.tensor_scalar(y[:, k, :], uc[0][:, k, :], dcol, None, ALU.mult)\
                                   .then_inc(yd_ready, 1)
                            else:
                                dve.wait_ge(yd_ready, at(6, b, k + 1))
                                dve.scalar_tensor_tensor(out=y[:, k, :], in0=uc[1][:, k, :], scalar=dcol,
                                                         in1=y[:, k, :], op0=ALU.mult, op1=ALU.add)\
                                   .then_inc(yd_ready, 1)
                    for d in range(2):
                        if d == 1:
                            dve.wait_ge(yd_ready, at(6, b, 6))
                        step_sizes(b, d)
                        before = None
                        for r, n, k in rows(d):
                            for kind, i in SLOTS[r] if layer1 else ():
                                item(kind, i, b, True)
                            input_row(b, r, n, k, d)
                            if before:
                                output_row(b, *before)
                            scan_row(b, r, d)
                            before = (r, n, k, d)
                            for kind, i in SLOTS[r] if layer1 else ():
                                item(kind, i, b, False)
                        output_row(b, *before)
                    for k in range(KT):
                        dve.wait_ge(y_done, at(ROWS, b, ROWS))
                        dve.wait_ge(ip_evac, at(12, b, 12))
                        dve.tensor_tensor(y[:, k, :], y[:, k, :], zs[:, k, :], ALU.mult).then_inc(yz_ready, 1)
                    for t in range(6):
                        m, c = t // 2, t % 2
                        toks = slice(c * HALF, (c + 1) * HALF)
                        dve.wait_ge(op_ready, at(6, b, t + 1))
                        dve.wait_ge(xres_ready, at(3, b, 3))
                        dve.wait_ge(out_dma, at(16, b, 0))
                        dve.scalar_tensor_tensor(out=xa[:, m, toks], in0=pW[:, t % 4, :], scalar=g_col,
                                                 in1=xres[:, m, toks], op0=ALU.mult, op1=ALU.add)\
                           .then_inc(xa_ready, 1)
                else:
                    for kind, i, _ in ITEMS:
                        item(kind, i, b, True)
                        item(kind, i, b, False)

            samples(dve, iteration)

        @block.gpsimd
        def _(pool):
            pool.memset(small[0:1, 32:33], 1.0).then_inc(prep_pool, 1)
            pool.memset(narrow[:, :], 0.0).then_inc(prep_pool, 1)
            pool.memset(stat[:, :, :], 0.0).then_inc(prep_pool, 1)

            def item(kind, n, b):
                a = b - 1
                if kind == "ln_scale":
                    for c in range(2):
                        toks = slice(c * HALF, (c + 1) * HALF)
                        pool.wait_ge(ln_rs, at(4, a, 2 * n + c + 1))
                        pool.tensor_tensor(lnx_of[n][:, :, toks], lnx_of[n][:, :, toks],
                                           prob[:, c * HALF:(c + 1) * HALF].unsqueeze(1).broadcast_to([128, KT, HALF]),
                                           ALU.mult).then_inc(ln_xn, 1)

            def iteration(b, layer0, layer1):
                if layer0:
                    for k in range(KT):
                        pool.wait_ge(loc_ready, at(3, b, k + 1))
                        pool.tensor_tensor(xres[:, k, :], xres[:, k, :], y[:, k, :], ALU.add).then_inc(xres_ready, 1)
                    for d in range(2):
                        for r, n, k in rows(d):
                            for kind, i in SLOTS[r] if layer1 else ():
                                item(kind, i, b)
                            pool.wait_ge(m2_done, at(ROWS, b, r + 1))
                            if r < KT:
                                pool.wait_ge(yd_ready, at(6, b, 6))
                            else:
                                pool.wait_ge(y_done, at(ROWS, b, r - 2))
                            pool.tensor_tensor(y[:, k, :], y[:, k, :], hb[r % 3][:, :], ALU.add).then_inc(y_done, 1)
                else:
                    for kind, i, _ in ITEMS:
                        item(kind, i, b)

            samples(pool, iteration)


def constants():
    import numpy as np

    c = np.zeros((128, 512), np.float32)
    c[:, 0:128] = np.eye(128)
    c[:, 128:256] = np.triu(np.full((128, 128), -1e30), 1)
    c[:, 256:384] = 1.0 / C
    c[0:96, 384:416] = np.tile(np.eye(32), (3, 1))
    k32 = np.zeros((KI, 2 * C), np.float32)
    ch = np.arange(C)
    member = (ch[:, None] // 12 == np.arange(KI)[None, :]).astype(np.float32)
    k32[:, 0:C] = member.T
    k32[0:12, C:] = (ch[None, :] % 12 == np.arange(12)[:, None])
    c = np.concatenate([c[:, 0:416], member.reshape(KT, 128, KI).transpose(1, 0, 2).reshape(128, KT * KI)], 1)
    return c, k32


def kernel(**inputs):
    import concourse.bacc as bacc
    import numpy as np
    from concourse.bass_utils import run_bass_kernel_spmd

    i0 = {n[8:]: np.asarray(v) for n, v in inputs.items() if n.startswith("L0_conv_")}
    at = {n[8:]: np.asarray(v) for n, v in inputs.items() if n.startswith("L1_attn_")}
    ff = {n[7:]: np.asarray(v) for n, v in inputs.items() if n.startswith("L1_ffn_")}
    k128, k32 = constants()
    xp = i0["x_proj_w"]
    arrays = {
        "x": np.asarray(inputs["x"]).reshape(NB, C, L),
        "chan": np.concatenate([
            np.stack([i0["norm_w"], i0["conv1d_b"], i0["dt_proj_b"], i0["D_param"], i0["dw_b"],
                      at["bq"], at["bk"], at["bv"], at["bo"]], 1),
            i0["conv1d_w"], i0["dw_w"].reshape(C, 9), i0["A_log"]], 1),
        "scal": np.stack([i0["scale_mod"], i0["res_scale"]], 1),
        "k128": k128,
        "k32": k32,
        "w_in": i0["in_proj_w"].T,
        "w_x": np.concatenate([xp[RANK:], xp[:RANK]], 0).T,
        "w_dt": i0["dt_proj_w"].T,
        "w_out": i0["out_proj_w"].T,
        "wq": at["Wq"], "wk": at["Wk"], "wv": at["Wv"], "wo": at["Wo"],
        "fc1": ff["c_fc_1"].T, "fc2": ff["c_fc_2"].T, "pr1": ff["c_proj_1"].T, "pr2": ff["c_proj_2"],
    }
    nc = bacc.Bacc("TRN2", target_bir_lowering=False, num_devices=1)
    feed, args = {}, []
    for name, a in arrays.items():
        a = np.ascontiguousarray(a)
        feed[f"in_{name}"] = a
        args.append(nc.dram_tensor(f"in_{name}", a.shape, mybir.dt.from_np(a.dtype), kind="ExternalInput").ap())
    out = nc.dram_tensor("out_x", (NB, C, L), F32, kind="ExternalOutput").ap()
    hybrid_block(nc, *args, out)
    r = run_bass_kernel_spmd(nc, [feed], core_ids=[0])
    return r.results[0]["out_x"].reshape(NB, C, HH, WW)
```

```python
from contextlib import ExitStack

import concourse.bass as bass
from concourse import mybir

F32 = mybir.dt.float32
BF16 = mybir.dt.bfloat16
ALU = mybir.AluOpType
ACT = mybir.ActivationFunctionType
AX = mybir.AxisListType.X

NB, C, HH, WW = 8, 384, 32, 32
L = HH * WW
KT = C // 128
HALF = L // 2
NS = 16
NTAP = 4
RANK = 24
NH, DH = 6, 64
QT = L // 128
FF = 1536
NF = FF // 128
KI = 32
WP = WW + 2
UP = L + 2 * (NTAP - 1)
ROWS = 2 * NS * KT
DROWS = NS * KT
VK = KT - 1
VROWS = 2 * NS * VK

(V_NW, V_CB, V_DTB, V_D, V_DWB, V_BQ, V_BK, V_BV, V_BO) = range(9)
V_CW, V_DW, V_A = 9, 13, 22
NV = V_A + NS

GROUPS = []
for _h in range(0, NH, 2):
    for _g in (_h, _h + 1):
        GROUPS += [[(_g, QT - 1, 0)]] + [[(_g, i, 0), (_g, QT - 2 - i, 128 * (i + 1))] for i in range(QT // 2 - 1)]
    GROUPS.append([(_h, QT // 2 - 1, 0), (_h + 1, QT // 2 - 1, HALF)])
NG = len(GROUPS)

NPJ = 20
FGRP = 3
NFG = NF // FGRP
ITEMS = (
    [("ln_mean", 0, 0.8), ("ln_var", 0, 0.9), ("ln_scale", 0, 0.9)]
    + [("proj", t, 0.75) for t in range(NPJ)]
    + [x for p in range(NG + 1) for x in (("scores", p, 0.9), ("values", p, 0.9))]
    + [("ctx_t", g, 0.4) for g in range(6)]
    + [("wo", t, 0.75) for t in range(6)]
    + [("ln_mean", 1, 0.8), ("ln_var", 1, 0.9), ("ln_scale", 1, 0.9), ("mlp_in", 0, 1.5)]
    + [x for c in range(2) for x in [("mlp", c * (NFG + 1) + q, 1.4) for q in range(NFG + 1)] + [("mlp_out", c, 1.0)]]
)


def slots():
    total = sum(w for _, _, w in ITEMS)
    out, at = [[] for _ in range(ROWS)], 0.0
    for kind, n, w in ITEMS:
        out[min(ROWS - 1, int(at * ROWS / total))].append((kind, n))
        at += w
    return out


SLOTS = slots()


def hybrid_block(nc, x, chan, scal, k128, k32, w_in, w_x, w_dt, w_out, wq, wk, wv, wo, fc1, fc2, pr1, pr2, out):
    with ExitStack() as ctx:
        def sb(name, shape, dt=F32):
            return ctx.enter_context(nc.sbuf_tensor(name, shape, dt))

        def sem(name):
            return ctx.enter_context(nc.semaphore(name))

        vec = sb("vec", [128, KT, NV])
        consts = sb("consts", [128, 256])
        ident, ones_c = consts[:, 0:128], consts[:, 128:256]
        sel_bf = sb("sel_bf", [128, 32], BF16)
        ident_bf = sb("ident_bf", [128, 128], BF16)
        causal_bf = sb("causal_bf", [128, 128], BF16)
        tiny = sb("tiny", [128, 8])
        rs_col, g_col, eps6, eps5, bq_s = tiny[:, 0:1], tiny[:, 1:2], tiny[:, 2:3], tiny[:, 3:4], tiny[:, 4:7]
        xp_w = sb("xp_w", [128, KT, 56])
        op_w = sb("op_w", [128, KT, C])
        q_w, k_w, v_w, o_w = (sb(n, [128, KT, C]) for n in ("q_w", "k_w", "v_w", "o_w"))
        mixed = sb("mixed", [128, FF])
        fc_w = mixed[0:KI, :]
        dt_w = [mixed[32:32 + RANK, 0:C], mixed[96:96 + RANK, 0:C]]
        kout_w = mixed[64:64 + KI, 0:C]
        pr_w = sb("pr_w", [128, NF, KI])
        kin_w = sb("kin_w", [128, KT, KI])
        small = sb("small", [128, 64])
        stat = sb("stat", [128, 3, 4])

        xres = sb("xres", [128, KT, L])
        delta = sb("delta", [128, KT, L])
        du_f = sb("du_f", [128, KT, L])
        uc_b = sb("uc_b", [128, KT, L])
        y = sb("y", [128, KT, L])
        zs = sb("zs", [128, KT, L])
        dA = [sb(f"dA{i}", [128, L]) for i in range(2)]
        hb = [sb(f"hb{i}", [128, L]) for i in range(3)]
        b_sb = sb("b_sb", [128, L])
        bc3 = [sb(f"bc3_{d}", [96, L], BF16) for d in range(2)]
        narrow = sb("narrow", [128, L])
        xr = narrow[0:KI, :]
        dtr = [narrow[32:32 + RANK, :], narrow[96:96 + RANK, :]]
        rr = narrow[64:64 + KI, :]

        early = du_f[:, 0, 0:256]

        xa = sb("xa", [128, KT, L])
        xn_area = sb("xn_area", [128, KT * L])
        area0 = sb("area0", [128, KT * HH * WP + KT * 2 * WP])
        area1 = sb("area1", [128, KT * UP])
        area2 = sb("area2", [128, KT * L])
        prob = sb("prob", [128, L])
        pt = sb("pt", [128, L])

        def tiled(area):
            return area[:, 0:KT * L].rearrange("p (k t) -> p k t", k=KT)

        ip_w = xn_area[:, 0:KT * 2 * C].rearrange("p (k e) -> p k e", k=KT)
        xnp = area0[:, :].rearrange("p (k h w) -> p k h w", k=KT, h=HH + 2)
        up = area1[:, :].rearrange("p (k t) -> p k t", k=KT)
        uc_f = tiled(area2)
        uc = [uc_f, uc_b]
        du = [du_f, uc_b]
        xn1, xn2 = tiled(xn_area), tiled(area1)
        sq_of = [tiled(area0), tiled(area2)]
        lnx_of = [xn1, xn2]
        qT, kT, ctxT = tiled(area0), tiled(area1), tiled(area0)
        vtok = area2[:, :].rearrange("p (j c) -> p j c", j=QT)
        ctxk = xn_area[:, :].rearrange("p (j c) -> p j c", j=QT)
        hid = area0[:, 0:2 * FGRP * HALF].rearrange("p (s f t) -> p s f t", s=2, f=FGRP)

        pB = ctx.enter_context(nc.psum_tensor("pB", [128, L], F32))
        pC = ctx.enter_context(nc.psum_tensor("pC", [128, L], F32))
        pW = ctx.enter_context(nc.psum_tensor("pW", [128, 4, HALF], F32))
        pS = pW[:, 0:2, :].rearrange("p b t -> p (b t)")

        consts_in, prep_act, prep_dve, prep_pe, prep_pool = (
            sem(n) for n in ("consts_in", "prep_act", "prep_dve", "prep_pe", "prep_pool"))
        x_in, win_in, out_dma = (sem(n) for n in ("x_in", "win_in", "out_dma"))
        pad_zero, sq_ready, ms_ready, ms_log, rstd_ready, xn_ready, ip_ready, ip_evac = (
            sem(n) for n in ("pad_zero", "sq_ready", "ms_ready", "ms_log", "rstd_ready", "xn_ready", "ip_ready",
                             "ip_evac"))
        dw_step, sig_ready, loc_ready, xres_ready, cv_step, uc_ready = (
            sem(n) for n in ("dw_step", "sig_ready", "loc_ready", "xres_ready", "cv_step", "uc_ready"))
        xd_ready, xd_evac, split_step, yd_ready = (sem(n) for n in ("xd_ready", "xd_evac", "split_step", "yd_ready"))
        dt_ready, relu_done, sp_abs, sp_exp, sp_ready, delta_ready, du_ready = (
            sem(n) for n in ("dt_ready", "relu_done", "sp_abs", "sp_exp", "sp_ready", "delta_ready", "du_ready"))
        b_ready, c_ready, bsb_ready, da_ready, m1_done, m1p_done, scan_done, m2_done, y_done = (
            sem(n) for n in ("b_ready", "c_ready", "bsb_ready", "da_ready", "m1_done", "m1p_done", "scan_done", "m2_done", "y_done"))
        yz_ready, op_ready, xa_ready = (sem(n) for n in ("yz_ready", "op_ready", "xa_ready"))
        ln_mean, ln_xc, ln_sq, ln_var, ln_log, ln_rs, ln_xn = (
            sem(n) for n in ("ln_mean", "ln_xc", "ln_sq", "ln_var", "ln_log", "ln_rs", "ln_xn"))
        pj_ready, pj_evac, s_ready, nmax_ready, p_ready, tr_ready, pt_ready, pv_done, rinv_ready, ctx_ready = (
            sem(n) for n in ("pj_ready", "pj_evac", "s_ready", "nmax_ready", "p_ready", "tr_ready", "pt_ready",
                             "pv_done", "rinv_ready", "ctx_ready"))
        ct_ready, ct_evac, wo_ready, wo_add = (sem(n) for n in ("ct_ready", "ct_evac", "wo_ready", "wo_add"))
        xr_ready, xr_evac, fc_ready, h_ready, r_done, r_evac, fo_ready, x2_ready = (
            sem(n) for n in ("xr_ready", "xr_evac", "fc_ready", "h_ready", "r_done", "r_evac", "fo_ready",
                             "x2_ready"))

        def at(per, b, n):
            v = b * per + n
            return max(v, 0) if isinstance(v, int) else v

        def samples(eng, iteration):
            iteration(0, True, False)
            with eng.Fori(1, NB) as b:
                iteration(b, True, True)
            iteration(NB, False, True)

        def rows(d):
            return [(d * DROWS + n * KT + k, n, k) for n in range(NS) for k in range(KT)]

        def flow(d, ap):
            return ap if d == 0 else ap[:, ::-1]

        block = ctx.enter_context(nc.Block())

        @block.sync
        def _(sp):
            def load_x(b):
                sp.wait_ge(xa_ready, at(6, b, 0))
                sp.dma_start(xres[:, :, :], x[b].rearrange("(k p) t -> p k t", p=128)).then_inc(x_in, 16)

            sp.dma_start(ip_w, w_in.rearrange("(k p) e -> p k e", p=128)).then_inc(win_in, 16)
            load_x(0)
            for dst, src in ((vec[:, :, :], chan.rearrange("(k p) v -> p k v", p=128)),
                             (consts[:, :], k128[:, 0:256]), (early[:, :], k128[:, 256:512]),
                             (small[0:1, 0:2], scal[:, :]),
                             (prob[0:KI, 0:2 * C], k32[:, :]),
                             (small[0:12, 2:3], fc2[:, :]),
                             (small[0:12, 3:4], pr2[:, :]),
                             (xp_w[:, :, :], w_x.rearrange("(k p) e -> p k e", p=128)),
                             (dt_w[0], w_dt[:, :]), (dt_w[1], w_dt[:, :]),
                             (op_w[:, :, :], w_out.rearrange("(k p) e -> p k e", p=128)),
                             (q_w[:, :, :], wq.rearrange("(k p) e -> p k e", p=128)),
                             (k_w[:, :, :], wk.rearrange("(k p) e -> p k e", p=128)),
                             (v_w[:, :, :], wv.rearrange("(k p) e -> p k e", p=128)),
                             (o_w[:, :, :], wo.rearrange("(k p) e -> p k e", p=128)),
                             (fc_w, fc1[:, :]),
                             (pr_w[:, :, :], pr1.rearrange("(f p) i -> p f i", p=128))):
                sp.dma_start(dst, src).then_inc(consts_in, 16)

            def iteration(b, layer0, layer1):
                if layer0 and not (isinstance(b, int) and b == 0):
                    load_x(b)
                if layer1:
                    if layer0:
                        sp.wait_ge(ct_evac, at(6, b, 0))
                        sp.dma_start(ip_w, w_in.rearrange("(k p) e -> p k e", p=128)).then_inc(win_in, 16)
                    sp.wait_ge(x2_ready, at(2, b, 0))
                    a = b - 1
                    sp.dma_start(out[a].rearrange("(k p) t -> p k t", p=128), xa[:, :, :]).then_inc(out_dma, 16)

            samples(sp, iteration)
            sp.wait_ge(out_dma, 16 * NB)
            sp.wait_ge(win_in, 16 * NB)

        NCONST = 17 * 16

        @block.tensor
        def _(pe):
            pe.wait_ge(consts_in, NCONST)
            rep = prob[0:12, C:2 * C]
            for k in range(KT):
                pe.matmul(pW[:, 0, k:k + 1], rep[:, 128 * k:128 * k + 128], small[0:12, 2:3], start=True, stop=True)
            pe.matmul(pW[0:KI, 1, 0:C], small[0:12, 3:4].broadcast_to([12, KI]), rep, start=True, stop=True)
            pe.wait_ge(prep_pool, 1)
            pe.matmul(pW[:, 2, 0:2], small[0:1, 32:33].broadcast_to([1, 128]), small[0:1, 0:2],
                      start=True, stop=True).then_inc(prep_pe, 1)
            pe.wait_ge(prep_dve, 1)

            def project(bank, w, cols, src, toks, done):
                for k in range(KT):
                    mm = pe.matmul(bank, w[:, k, cols], src[:, k, toks], start=(k == 0), stop=(k == KT - 1))
                mm.then_inc(done, 1)

            def average(bank, src, toks, done):
                for k in range(KT):
                    mm = pe.matmul(bank, ones_c, src[:, k, toks], start=(k == 0), stop=(k == KT - 1))
                mm.then_inc(done, 1)

            def step_sizes(b, d):
                for k in range(KT):
                    bank = (pB, pC)[k % 2]
                    if k == 0:
                        pe.wait_ge(xd_evac, at(4, b, 2 + 2 * d))
                        pe.wait_ge(m2_done, at(ROWS, b, DROWS * d))
                        pe.wait_ge(y_done, at(ROWS, b, DROWS * d - 3))
                    if k == 2:
                        pe.wait_ge(relu_done, at(6, b, 3 * d + 1))
                        pe.wait_ge(sp_abs, at(6, b, 3 * d + 1))
                    for c in range(2):
                        mm = pe.matmul(bank[:, c * HALF:(c + 1) * HALF], dt_w[d][:, 128 * k:128 * k + 128],
                                       dtr[d][:, c * HALF:(c + 1) * HALF], start=True, stop=True)
                    mm.then_inc(dt_ready, 1)

            def spread(b, d, n, bank, row, done):
                for c in range(2):
                    mm = pe.matmul(bank[:, c * HALF:(c + 1) * HALF], sel_bf[0:96, row:row + 1].broadcast_to([96, 128]),
                                   bc3[d][:, c * HALF:(c + 1) * HALF], start=True, stop=True)
                mm.then_inc(done, 1)

            def spread_b(b, d, n):
                if n == 0:
                    pe.wait_ge(split_step, at(10, b, 5 * (d + 1)))
                    pe.wait_ge(delta_ready, at(6, b, 3 * (d + 1)))
                else:
                    pe.wait_ge(m1_done, at(VROWS, b, VK * (NS * d + n)))
                spread(b, d, n, pB, n, b_ready)

            def spread_c(b, d, n):
                if n:
                    pe.wait_ge(m2_done, at(ROWS, b, DROWS * d + KT * n))
                spread(b, d, n, pC, NS + n, c_ready)

            def item(kind, n, b):
                a = b - 1
                if kind == "ln_mean":
                    for c in range(2):
                        if n == 0:
                            pe.wait_ge(xa_ready, at(6, a, 6))
                            if isinstance(b, int):
                                pe.wait_ge(xd_evac, at(4, NB, 0))
                            else:
                                pe.wait_ge(xd_evac, at(4, b, 4))
                        else:
                            pe.wait_ge(wo_add, at(6, a, 6))
                        average(pW[:, 2 * c, :], xa, slice(c * HALF, (c + 1) * HALF), ln_mean)
                elif kind == "ln_var":
                    for c in range(2):
                        pe.wait_ge(ln_sq, at(4, a, 2 * n + c + 1))
                        average(pW[:, 2 * c + 1, :], sq_of[n],
                                slice(c * HALF, (c + 1) * HALF), ln_var)
                elif kind == "proj":
                    pe.wait_ge(ln_xn, at(4, a, 2))
                    if n >= 4:
                        pe.wait_ge(pj_evac, at(NPJ, a, n - 3))
                    bank = pW[:, n % 4, :]
                    if n < 12:
                        m, c = n % 6 // 2, n % 2
                        project(bank, (q_w, k_w)[n // 6], slice(128 * m, 128 * m + 128), xn1,
                                slice(c * HALF, (c + 1) * HALF), pj_ready)
                    else:
                        j = n - 12
                        for k in range(KT):
                            mm = pe.matmul(bank[:, 0:C], xn1[:, k, 128 * j:128 * j + 128], v_w[:, k, :],
                                           start=(k == 0), stop=(k == KT - 1))
                        mm.then_inc(pj_ready, 1)
                elif kind == "scores":
                    if n < NG:
                        pe.wait_ge(pj_evac, at(NPJ, a, NPJ))
                        if n:
                            pe.wait_ge(p_ready, at(NG, a, n))
                        for h, i, c0 in GROUPS[n]:
                            p0, end = DH * (h % 2), c0 + 128 * (i + 1)
                            q = qT[p0:p0 + DH, h // 2, 128 * i:128 * i + 128]
                            for lo, hi in ((c0, min(end, HALF)), (max(c0, HALF), end)):
                                if lo < hi:
                                    pe.matmul(pS[:, lo:hi], q, kT[p0:p0 + DH, h // 2, lo - c0:hi - c0],
                                              start=True, stop=hi != end)
                            mm = pe.matmul(pS[:, end - 128:end], ident_bf[:, :], causal_bf[:, :],
                                           start=False, stop=True)
                        mm.then_inc(s_ready, 1)
                    if n:
                        g = n - 1
                        pe.wait_ge(p_ready, at(NG, a, g + 1))
                        for half in range(2):
                            if g:
                                pe.wait_ge(pt_ready, at(2 * NG, a, 2 * g - 1 + half))
                            if g and half:
                                pe.wait_ge(ctx_ready, at(NG, a, g))
                            for j in range(4):
                                mm = pe.transpose(pW[:, 2 + half, 128 * j:128 * j + 128],
                                                  prob[:, half * HALF + 128 * j:half * HALF + 128 * j + 128], ident)
                            mm.then_inc(tr_ready, 1)
                elif kind == "values":
                    if n:
                        g = n - 1
                        pe.wait_ge(pt_ready, at(2 * NG, a, 2 * g + 2))
                        for t, (h, i, c0) in enumerate(GROUPS[g]):
                            for j in range(i + 1):
                                mm = pe.matmul(pW[:, 3, DH * t:DH * t + DH], pt[:, c0 + 128 * j:c0 + 128 * j + 128],
                                               vtok[:, j, DH * h:DH * h + DH], start=(j == 0), stop=(j == i))
                        mm.then_inc(pv_done, 1)
                elif kind == "ctx_t":
                    m, c = n // 2, n % 2
                    pe.wait_ge(ctx_ready, at(NG, a, NG))
                    if n >= 4:
                        pe.wait_ge(ct_evac, at(6, a, n - 3))
                    for j in range(4):
                        mm = pe.transpose(pW[:, n % 4, 128 * j:128 * j + 128],
                                          ctxk[:, 4 * c + j, 128 * m:128 * m + 128], ident)
                    mm.then_inc(ct_ready, 1)
                elif kind == "wo":
                    m, c = n // 2, n % 2
                    pe.wait_ge(ct_evac, at(6, a, 6))
                    if n >= 4:
                        pe.wait_ge(wo_add, at(6, a, n - 3))
                    project(pW[:, n % 4, :], o_w, slice(128 * m, 128 * m + 128), ctxT,
                            slice(c * HALF, (c + 1) * HALF), wo_ready)
                elif kind == "mlp_in":
                    pe.wait_ge(ln_xn, at(4, a, 4))
                    for c in range(2):
                        project(pW[0:KI, c, :], kin_w, slice(0, KI), xn2, slice(c * HALF, (c + 1) * HALF), xr_ready)
                elif kind == "mlp":
                    c, q = n // (NFG + 1), n % (NFG + 1)
                    g = c * NFG + q
                    toks = slice(c * HALF, (c + 1) * HALF)

                    def hidden():
                        pe.wait_ge(xr_evac, at(2, a, 2))
                        if g:
                            pe.wait_ge(h_ready, at(2 * NFG, a, g))
                        if q == 0 and c:
                            pe.wait_ge(x2_ready, at(2, a, c))
                        for f in range(FGRP):
                            ft = FGRP * q + f
                            mm = pe.matmul(pW[:, f, :], fc_w[:, 128 * ft:128 * ft + 128], xr[:, toks],
                                           start=True, stop=True)
                        mm.then_inc(fc_ready, 1)

                    if q < NFG:
                        hidden()
                    if q >= 1:
                        pe.wait_ge(h_ready, at(2 * NFG, a, g))
                        if q == 1 and c:
                            pe.wait_ge(r_evac, at(2, a, c))
                        for f in range(FGRP):
                            ft = FGRP * (q - 1) + f
                            mm = pe.matmul(pW[0:KI, 3, :], pr_w[:, ft, :], hid[:, (g - 1) % 2, f, :],
                                           start=(ft == 0), stop=(ft == NF - 1))
                        mm.then_inc(r_done, 1)
                elif kind == "mlp_out":
                    pe.wait_ge(r_evac, at(2, a, n + 1))
                    for m in range(KT):
                        mm = pe.matmul(pW[:, m, :], kout_w[:, 128 * m:128 * m + 128],
                                       rr[:, n * HALF:(n + 1) * HALF], start=True, stop=True)
                    mm.then_inc(fo_ready, 1)

            def iteration(b, layer0, layer1):
                if layer0:
                    pe.wait_ge(m2_done, at(ROWS, b, 0))
                    pe.wait_ge(sq_ready, at(3, b, 3))
                    for c in range(2):
                        average(pB[:, c * HALF:(c + 1) * HALF], uc_f,
                                slice(c * HALF, (c + 1) * HALF), ms_ready)
                    pe.wait_ge(xn_ready, at(3, b, 3))
                    if isinstance(b, int):
                        pe.wait_ge(win_in, 16)
                    else:
                        pe.wait_ge(win_in, at(16, b, 0))
                    pe.wait_ge(xa_ready, at(6, b, 0))
                    for t in range(12):
                        m, c = t // 2, t % 2
                        if t >= 4:
                            pe.wait_ge(ip_evac, at(12, b, t - 3))
                        for k in range(KT):
                            mm = pe.matmul(pW[:, t % 4, :], ip_w[:, k, 128 * m:128 * m + 128],
                                           xnp[:, k, 1 + 16 * c:17 + 16 * c, 1:1 + WW],
                                           start=(k == 0), stop=(k == KT - 1))
                        mm.then_inc(ip_ready, 1)
                    pe.wait_ge(ip_evac, at(12, b, 12))
                    for d in range(2):
                        pe.wait_ge(uc_ready, at(6, b, 3 * d + 3))
                        for c in range(2):
                            for k in range(KT):
                                mm = pe.matmul(pW[0:56, 2 * d + c, :], xp_w[:, k, :],
                                               uc[d][:, k, c * HALF:(c + 1) * HALF], start=(k == 0), stop=(k == KT - 1))
                        mm.then_inc(xd_ready, 1)
                if layer0:
                    for d in range(2):
                        step_sizes(b, d)
                        spread_b(b, d, 0)
                        for r, n, k in rows(d):
                            if layer1:
                                for kind, i in SLOTS[r]:
                                    item(kind, i, b)
                            if k == 1 and n + 1 < NS:
                                spread_b(b, d, n + 1)
                            if k == 0:
                                spread_c(b, d, n)
                    for t in range(6):
                        m, c = t // 2, t % 2
                        if t == 0:
                            pe.wait_ge(yz_ready, at(3, b, 3))
                            pe.wait_ge(x2_ready, at(2, b, 0))
                        if t >= 4:
                            pe.wait_ge(xa_ready, at(6, b, t - 3))
                        project(pW[:, t % 4, :], op_w, slice(128 * m, 128 * m + 128), y,
                                slice(c * HALF, (c + 1) * HALF), op_ready)
                else:
                    for kind, i, _ in ITEMS:
                        item(kind, i, b)

            samples(pe, iteration)

        @block.scalar
        def _(act):
            act.wait_ge(consts_in, NCONST)
            act.wait_ge(prep_pool, 3)
            act.activation(vec[:, :, V_A:V_A + NS], vec[:, :, V_A:V_A + NS], ACT.Exp).then_inc(prep_act, 1)
            act.copy(ident_bf[:, :], ident)
            act.copy(causal_bf[:, :], early[:, 0:128])
            act.copy(sel_bf[:, :], early[:, 128:160]).then_inc(prep_act, 1)
            act.wait_ge(prep_dve, 1)

            def step_sizes(b, d):
                for k in range(KT):
                    t = dA[k % 2]
                    if k < 2:
                        act.wait_ge(scan_done, at(ROWS, b, DROWS * d))
                        act.wait_ge(xn_ready, at(3, b, 3))
                    else:
                        act.wait_ge(delta_ready, at(6, b, 3 * d + 1))
                    act.wait_ge(dt_ready, at(6, b, 3 * d + k + 1))
                    act.activation(t[:, :], (pB, pC)[k % 2][:, :], ACT.Abs,
                                   bias=vec[:, k, V_DTB:V_DTB + 1]).then_inc(sp_abs, 1)
                    act.wait_ge(sp_abs, at(6, b, 3 * d + k + 1))
                    act.activation(t[:, :], t[:, :], ACT.Exp, scale=-1.0).then_inc(sp_exp, 1)
                    act.wait_ge(sp_exp, at(6, b, 3 * d + k + 1))
                    act.activation(t[:, :], t[:, :], ACT.Ln, bias=1.0).then_inc(sp_ready, 1)

            def decay(b, r):
                d, k = r // DROWS, r % KT
                n = r % DROWS // KT
                act.wait_ge(scan_done, at(ROWS, b, r - 1))
                if r % DROWS < KT:
                    act.wait_ge(delta_ready, at(6, b, 3 * d + 3))
                act.activation(dA[r % 2][:, :], delta[:, k, :], ACT.Exp,
                               scale=vec[:, k, V_A + n:V_A + n + 1]).then_inc(da_ready, 1)

            def copy_b(b, d, n):
                act.wait_ge(b_ready, at(2 * NS, b, NS * d + n + 1))
                act.wait_ge(m1p_done, at(2 * NS, b, NS * d + n))
                act.copy(b_sb[:, :], pB[:, :]).then_inc(bsb_ready, 1)

            def item(kind, n, b, early):
                a = b - 1
                if kind == "ln_var" and early:
                    for c in range(2):
                        if n == 0:
                            if isinstance(b, int):
                                act.wait_ge(du_ready, at(6, NB, 0))
                            else:
                                act.wait_ge(du_ready, at(6, b, 3))
                        act.wait_ge(ln_xc, at(4, a, 2 * n + c + 1))
                        toks = slice(c * HALF, (c + 1) * HALF)
                        act.activation(sq_of[n][:, :, toks], lnx_of[n][:, :, toks], ACT.Square).then_inc(ln_sq, 1)
                elif kind == "ln_scale" and early:
                    for c in range(2):
                        act.wait_ge(ln_var, at(4, a, 2 * n + c + 1))
                        act.activation(prob[:, c * HALF:(c + 1) * HALF], pW[:, 2 * c + 1, :], ACT.Ln,
                                       bias=eps5).then_inc(ln_log, 1)
                    for c in range(2):
                        act.wait_ge(ln_log, at(4, a, 2 * n + c + 1))
                        act.activation(prob[:, c * HALF:(c + 1) * HALF], prob[:, c * HALF:(c + 1) * HALF], ACT.Exp,
                                       scale=-0.5).then_inc(ln_rs, 1)
                elif kind == "proj" and not early:
                    act.wait_ge(pj_ready, at(NPJ, a, n + 1))
                    act.wait_ge(ln_var, at(4, a, 2))
                    bank = pW[:, n % 4, :]
                    if n < 12:
                        m, c = n % 6 // 2, n % 2
                        toks = slice(c * HALF, (c + 1) * HALF)
                        if n < 6:
                            ev = act.activation(qT[:, m, toks], bank, ACT.Identity, bias=bq_s[:, m:m + 1], scale=0.125)
                        else:
                            ev = act.activation(kT[:, m, toks], bank, ACT.Identity, bias=vec[:, m, V_BK:V_BK + 1])
                    else:
                        ev = act.copy(vtok[:, n - 12, :], bank[:, 0:C])
                    ev.then_inc(pj_evac, 1)
                elif kind == "values" and early:
                    if n:
                        g = n - 1
                        for half in range(2):
                            act.wait_ge(tr_ready, at(2 * NG, a, 2 * g + half + 1))
                            if g:
                                act.wait_ge(pv_done, at(NG, a, g))
                            act.copy(pt[:, half * HALF:(half + 1) * HALF], pW[:, 2 + half, :]).then_inc(pt_ready, 1)
                    if n < NG:
                        act.wait_ge(nmax_ready, at(NG, a, n + 1))
                        if n:
                            act.wait_ge(tr_ready, at(2 * NG, a, 2 * n))
                        else:
                            act.wait_ge(ln_xn, at(4, a, 2))
                        if n >= 2:
                            act.wait_ge(ctx_ready, at(NG, a, n - 1))
                        for t, (h, i, c0) in enumerate(GROUPS[n]):
                            st = 2 * (n % 2) + t
                            end = c0 + 128 * (i + 1)
                            ex = act.activation(prob[:, c0:end], pS[:, c0:end], ACT.Exp, bias=stat[:, 0, st:st + 1],
                                                accum_out=stat[:, 1, st:st + 1])
                        ex.then_inc(p_ready, 1)
                elif kind == "ctx_t" and not early:
                    m, c = n // 2, n % 2
                    act.wait_ge(ct_ready, at(6, a, n + 1))
                    act.activation(ctxT[:, m, c * HALF:(c + 1) * HALF], pW[:, n % 4, :], ACT.Identity,
                                   bias=vec[:, m, V_BV:V_BV + 1]).then_inc(ct_evac, 1)
                elif kind == "mlp_in" and not early:
                    for c in range(2):
                        act.wait_ge(xr_ready, at(2, a, c + 1))
                        act.copy(xr[:, c * HALF:(c + 1) * HALF], pW[0:KI, c, :]).then_inc(xr_evac, 1)
                elif kind == "mlp" and not early:
                    c, q = n // (NFG + 1), n % (NFG + 1)
                    g = c * NFG + q
                    if q < NFG:
                        act.wait_ge(fc_ready, at(2 * NFG, a, g + 1))
                        if g >= 2:
                            act.wait_ge(r_done, at(2 * NFG, a, g - 1))
                        act.activation(hid[:, g % 2, :, :], pW[:, 0:FGRP, :], ACT.Gelu).then_inc(h_ready, 1)
                    else:
                        act.wait_ge(r_done, at(2 * NFG, a, g))
                        act.copy(rr[:, c * HALF:(c + 1) * HALF], pW[0:KI, 3, :]).then_inc(r_evac, 1)

            def iteration(b, layer0, layer1):
                if layer0:
                    act.wait_ge(xa_ready, at(6, b, 0))
                    for k in range(KT):
                        act.wait_ge(x_in, at(16, b, 16))
                        act.activation(uc_f[:, k, :], xres[:, k, :], ACT.Square).then_inc(sq_ready, 1)
                    act.wait_ge(ms_ready, at(2, b, 2))
                    act.wait_ge(scan_done, at(ROWS, b, 0))
                    act.activation(dA[0][:, :], pB[:, :], ACT.Ln, bias=eps6).then_inc(ms_log, 1)
                    act.wait_ge(ms_log, at(1, b, 1))
                    act.activation(dA[0][:, :], dA[0][:, :], ACT.Exp, scale=-0.5).then_inc(rstd_ready, 1)
                    for t in range(6):
                        m, c = t // 2, t % 2
                        act.wait_ge(ip_ready, at(12, b, t + 1))
                        act.wait_ge(pad_zero, at(6, b, 6))
                        act.copy(up[:, m, NTAP - 1 + c * HALF:NTAP - 1 + (c + 1) * HALF],
                                 pW[:, t % 4, :]).then_inc(ip_evac, 1)
                    for t in range(6, 12):
                        m, c = t // 2 - 3, t % 2
                        act.wait_ge(ip_ready, at(12, b, t + 1))
                        act.wait_ge(yz_ready, at(3, b, 0))
                        act.activation(zs[:, m, c * HALF:(c + 1) * HALF], pW[:, t % 4, :], ACT.Silu).then_inc(ip_evac, 1)
                    for k in range(KT):
                        act.wait_ge(dw_step, at(27, b, 24 + k + 1))
                        act.activation(y[:, k, :], y[:, k, :], ACT.Sigmoid).then_inc(sig_ready, 1)
                    for d in range(2):
                        for k in range(KT):
                            act.wait_ge(cv_step, at(24, b, 12 * d + 9 + k + 1))
                            act.activation(uc[d][:, k, :], uc[d][:, k, :], ACT.Silu,
                                           bias=vec[:, k, V_CB:V_CB + 1]).then_inc(uc_ready, 1)
                    for d in range(2):
                        act.wait_ge(xd_ready, at(2, b, d + 1))
                        act.wait_ge(y_done, at(ROWS, b, 0))
                        act.copy(hb[d][0:32, :], pW[0:32, 2 * d:2 * d + 2, :].rearrange("p b t -> p (b t)"))\
                            .then_inc(xd_evac, 1)
                        act.copy(dtr[d], pW[32:56, 2 * d:2 * d + 2, :].rearrange("p b t -> p (b t)"))\
                            .then_inc(xd_evac, 1)
                    for d in range(2):
                        step_sizes(b, d)
                        copy_b(b, d, 0)
                        decay(b, DROWS * d)
                        for r, n, k in rows(d):
                            for kind, i in SLOTS[r] if layer1 else ():
                                item(kind, i, b, True)
                            if r + 1 < DROWS * (d + 1):
                                decay(b, r + 1)
                            if k == 2 and n + 1 < NS:
                                copy_b(b, d, n + 1)
                            for kind, i in SLOTS[r] if layer1 else ():
                                item(kind, i, b, False)
                else:
                    for kind, i, _ in ITEMS:
                        item(kind, i, b, True)
                        item(kind, i, b, False)

            samples(act, iteration)

        @block.vector
        def _(dve):
            dve.memset(eps6, 1e-6)
            dve.memset(eps5, 1e-5)
            dve.wait_ge(prep_act, 2)
            dve.tensor_scalar(vec[:, :, V_A:V_A + NS], vec[:, :, V_A:V_A + NS], -1.0, None, ALU.mult)
            dve.tensor_scalar(bq_s, vec[:, :, V_BQ], 0.125, None, ALU.mult)
            dve.wait_ge(prep_pe, 1)
            for k in range(KT):
                dve.tensor_scalar(kin_w[:, k, :], early[:, 160 + KI * k:192 + KI * k],
                                  pW[:, 0, k:k + 1], None, ALU.mult)
            dve.tensor_tensor(kout_w, prob[0:KI, 0:C], pW[0:KI, 1, 0:C], ALU.mult)
            dve.tensor_copy(small[:, 8:10], pW[:, 2, 0:2]).then_inc(prep_dve, 0 + 1)
            dve.wait_ge(prep_dve, 1)
            dve.tensor_copy(rs_col, small[:, 9:10])
            dve.tensor_tensor(g_col, small[:, 8:9], small[:, 9:10], ALU.mult).then_inc(prep_dve, 1)
            dve.wait_ge(prep_dve, 2)

            def step_sizes(b, d):
                for k in range(KT):
                    dve.wait_ge(sp_abs, at(6, b, 3 * d + k + 1))
                    dve.wait_ge(da_ready, at(ROWS, b, DROWS * d))
                    dve.tensor_scalar(delta[:, k, :], (pB, pC)[k % 2][:, :], vec[:, k, V_DTB:V_DTB + 1], 0.0,
                                      ALU.add, ALU.max).then_inc(relu_done, 1)
                    dve.wait_ge(relu_done, at(6, b, 3 * d + k + 1))
                    dve.wait_ge(sp_ready, at(6, b, 3 * d + k + 1))
                    dve.tensor_tensor(delta[:, k, :], delta[:, k, :], dA[k % 2][:, :], ALU.add)\
                       .then_inc(delta_ready, 1)
                for k in range(KT):
                    dve.wait_ge(delta_ready, at(6, b, 3 * d + k + 1))
                    dve.wait_ge(m1_done, at(VROWS, b, VK * NS * d))
                    dve.wait_ge(m1p_done, at(2 * NS, b, NS * d))
                    dve.tensor_tensor(du[d][:, k, :], delta[:, k, :], uc[d][:, k, :], ALU.mult)\
                       .then_inc(du_ready, 1)

            def input_row(b, r, n, k, d):
                if k == 0:
                    dve.wait_ge(bsb_ready, at(2 * NS, b, NS * d + n + 1))
                dve.wait_ge(y_done, at(ROWS, b, r - 2))
                if n == 0:
                    dve.wait_ge(du_ready, at(6, b, 3 * d + k + 1))
                    dve.wait_ge(split_step, at(10, b, 10))
                dve.tensor_tensor(hb[r % 3][:, :], du[d][:, k, :], pB[:, :], ALU.mult).then_inc(m1_done, 1)

            def scan_row(b, r, n, k, d):
                dve.wait_ge(da_ready, at(ROWS, b, r + 1))
                if k < VK:
                    dve.wait_ge(m1_done, at(VROWS, b, VK * (NS * d + n) + k + 1))
                else:
                    dve.wait_ge(m1p_done, at(2 * NS, b, NS * d + n + 1))
                buf = hb[r % 3]
                dve.tensor_tensor_scan(flow(d, buf[:, :]), flow(d, dA[r % 2][:, :]), flow(d, buf[:, :]), 0.0,
                                       ALU.mult, ALU.add).then_inc(scan_done, 1)

            def output_row(b, r, n, k, d):
                if k == 0:
                    dve.wait_ge(c_ready, at(2 * NS, b, NS * d + n + 1))
                dve.wait_ge(scan_done, at(ROWS, b, r + 1))
                dve.tensor_tensor(hb[r % 3][:, :], hb[r % 3][:, :], pC[:, :], ALU.mult).then_inc(m2_done, 1)

            def item(kind, n, b, early):
                a = b - 1
                if kind == "ln_mean" and not early:
                    for c in range(2):
                        toks = slice(c * HALF, (c + 1) * HALF)
                        if n == 0:
                            if isinstance(b, int):
                                dve.wait_ge(ip_ready, at(12, NB, 0))
                            else:
                                dve.wait_ge(ip_ready, at(12, b, 12))
                        dve.wait_ge(ln_mean, at(4, a, 2 * n + c + 1))
                        dve.tensor_tensor(lnx_of[n][:, :, toks], xa[:, :, toks],
                                          pW[:, 2 * c:2 * c + 1, :].broadcast_to([128, KT, HALF]),
                                          ALU.subtract).then_inc(ln_xc, 1)
                elif kind == "values" and early and n < NG:
                    dve.wait_ge(s_ready, at(NG, a, n + 1))
                    if n >= 2:
                        dve.wait_ge(p_ready, at(NG, a, n - 1))
                    for t, (h, i, c0) in enumerate(GROUPS[n]):
                        st = 2 * (n % 2) + t
                        mx = dve.tensor_reduce(stat[:, 0, st:st + 1], pS[:, c0:c0 + 128 * (i + 1)], AX, ALU.max,
                                               negate=True)
                    mx.then_inc(nmax_ready, 1)
                elif kind == "values" and not early and n:
                    g = n - 1
                    st, nt = 2 * (g % 2), len(GROUPS[g])
                    dve.wait_ge(p_ready, at(NG, a, g + 1))
                    dve.reciprocal(stat[:, 2, st:st + nt], stat[:, 1, st:st + nt]).then_inc(rinv_ready, 1)
                    dve.wait_ge(rinv_ready, at(NG, a, g + 1))
                    dve.wait_ge(pv_done, at(NG, a, g + 1))
                    for t, (h, i, c0) in enumerate(GROUPS[g]):
                        cx = dve.tensor_scalar(ctxk[:, i, DH * h:DH * h + DH], pW[:, 3, DH * t:DH * t + DH],
                                               stat[:, 2, st + t:st + t + 1], None, ALU.mult)
                    cx.then_inc(ctx_ready, 1)
                elif kind == "wo" and not early:
                    m, c = n // 2, n % 2
                    toks = slice(c * HALF, (c + 1) * HALF)
                    dve.wait_ge(wo_ready, at(6, a, n + 1))
                    dve.scalar_tensor_tensor(out=xa[:, m, toks], in0=pW[:, n % 4, :], scalar=vec[:, m, V_BO:V_BO + 1],
                                             in1=xa[:, m, toks], op0=ALU.add, op1=ALU.add).then_inc(wo_add, 1)
                elif kind == "mlp_out" and not early:
                    toks = slice(n * HALF, (n + 1) * HALF)
                    dve.wait_ge(fo_ready, at(2, a, n + 1))
                    dve.wait_ge(wo_add, at(6, a, 6))
                    dve.tensor_tensor(xa[:, :, toks], xa[:, :, toks], pW[:, 0:3, :], ALU.add).then_inc(x2_ready, 1)

            def iteration(b, layer0, layer1):
                if layer0:
                    dve.wait_ge(xa_ready, at(6, b, 0))
                    for border in (xnp[:, :, 0, :], xnp[:, :, HH + 1, :], xnp[:, :, 1:1 + HH, 0:1],
                                   xnp[:, :, 1:1 + HH, WW + 1:WP], up[:, :, 0:NTAP - 1], up[:, :, UP - NTAP + 1:UP]):
                        dve.memset(border, 0.0).then_inc(pad_zero, 1)
                    dve.wait_ge(x_in, at(16, b, 16))
                    dve.wait_ge(pad_zero, at(6, b, 6))
                    for k in range(KT):
                        dve.wait_ge(rstd_ready, at(1, b, 1))
                        dve.scalar_tensor_tensor(out=xnp[:, k, 1:1 + HH, 1:1 + WW],
                                                 in0=xres[:, k, :].rearrange("p (h w) -> p h w", w=WW),
                                                 scalar=vec[:, k, V_NW:V_NW + 1],
                                                 in1=dA[0][:, :].rearrange("p (h w) -> p h w", w=WW),
                                                 op0=ALU.mult, op1=ALU.mult).then_inc(xn_ready, 1)
                    dve.wait_ge(op_ready, at(6, b, 0))
                    for j in range(9):
                        for k in range(KT):
                            step = KT * j + k
                            win = xnp[:, k, j // 3:j // 3 + HH, j % 3:j % 3 + WW]
                            acc = y[:, k, :].rearrange("p (h w) -> p h w", w=WW)
                            w = vec[:, k, V_DW + j:V_DW + j + 1]
                            if j == 0:
                                dve.wait_ge(xn_ready, at(3, b, k + 1))
                                dve.tensor_scalar(acc, win, w, vec[:, k, V_DWB:V_DWB + 1], ALU.mult, ALU.add)\
                                   .then_inc(dw_step, 1)
                            else:
                                dve.wait_ge(dw_step, at(27, b, step - 2))
                                dve.scalar_tensor_tensor(out=acc, in0=win, scalar=w, in1=acc, op0=ALU.mult,
                                                         op1=ALU.add).then_inc(dw_step, 1)
                    for d in range(2):
                        for j in range(NTAP):
                            for k in range(KT):
                                step = 12 * d + KT * j + k
                                off = j if d == 0 else 2 * (NTAP - 1) - j
                                src, w = up[:, k, off:off + L], vec[:, k, V_CW + j:V_CW + j + 1]
                                if j == 0:
                                    dve.wait_ge(ip_evac, at(12, b, 2 * k + 2))
                                    dve.wait_ge(ms_ready, at(2, b, 2))
                                    dve.wait_ge(m1_done, at(VROWS, b, 0))
                                    dve.wait_ge(m1p_done, at(2 * NS, b, 0))
                                    dve.tensor_scalar(uc[d][:, k, :], src, w, None, ALU.mult).then_inc(cv_step, 1)
                                else:
                                    dve.wait_ge(cv_step, at(24, b, step - 2))
                                    dve.scalar_tensor_tensor(out=uc[d][:, k, :], in0=src, scalar=w,
                                                             in1=uc[d][:, k, :], op0=ALU.mult, op1=ALU.add)\
                                       .then_inc(cv_step, 1)
                    for k in range(KT):
                        dve.wait_ge(sig_ready, at(3, b, k + 1))
                        acc = y[:, k, :].rearrange("p (h w) -> p h w", w=WW)
                        dve.scalar_tensor_tensor(out=acc, in0=acc, scalar=rs_col, in1=xnp[:, k, 1:1 + HH, 1:1 + WW],
                                                 op0=ALU.mult, op1=ALU.mult).then_inc(loc_ready, 1)
                    low = hb[2][0:32, 0:HALF].bitcast(BF16)
                    for d in range(2):
                        rest, parts = hb[d][0:32, :], bc3[d]
                        dve.wait_ge(xd_evac, at(4, b, 2 * d + 1))
                        dve.wait_ge(c_ready, at(2 * NS, b, 0))
                        dve.tensor_copy(parts[0:32, :], rest).then_inc(split_step, 1)
                        dve.wait_ge(split_step, at(10, b, 5 * d + 1))
                        dve.tensor_tensor(rest, rest, parts[0:32, :], ALU.subtract).then_inc(split_step, 1)
                        dve.wait_ge(split_step, at(10, b, 5 * d + 2))
                        dve.tensor_copy(low, rest).then_inc(split_step, 1)
                        dve.wait_ge(split_step, at(10, b, 5 * d + 3))
                        dve.tensor_tensor(parts[64:96, :], rest, low, ALU.subtract).then_inc(split_step, 1)
                        dve.tensor_copy(parts[32:64, :], low).then_inc(split_step, 1)
                    for d in range(2):
                        for k in range(KT):
                            dve.wait_ge(uc_ready, at(6, b, 3 * d + k + 1))
                            dcol = vec[:, k, V_D:V_D + 1]
                            if d == 0:
                                dve.wait_ge(xres_ready, at(3, b, k + 1))
                                dve.tensor_scalar(y[:, k, :], uc[0][:, k, :], dcol, None, ALU.mult)\
                                   .then_inc(yd_ready, 1)
                            else:
                                dve.wait_ge(yd_ready, at(6, b, k + 1))
                                dve.scalar_tensor_tensor(out=y[:, k, :], in0=uc[1][:, k, :], scalar=dcol,
                                                         in1=y[:, k, :], op0=ALU.mult, op1=ALU.add)\
                                   .then_inc(yd_ready, 1)
                    for d in range(2):
                        if d == 1:
                            dve.wait_ge(yd_ready, at(6, b, 6))
                        step_sizes(b, d)
                        before = None
                        for r, n, k in rows(d):
                            for kind, i in SLOTS[r] if layer1 else ():
                                item(kind, i, b, True)
                            if k < VK:
                                input_row(b, r, n, k, d)
                            if before:
                                output_row(b, *before)
                            scan_row(b, r, n, k, d)
                            before = (r, n, k, d)
                            for kind, i in SLOTS[r] if layer1 else ():
                                item(kind, i, b, False)
                        output_row(b, *before)
                    for k in range(KT):
                        dve.wait_ge(y_done, at(ROWS, b, ROWS))
                        dve.wait_ge(ip_evac, at(12, b, 12))
                        dve.tensor_tensor(y[:, k, :], y[:, k, :], zs[:, k, :], ALU.mult).then_inc(yz_ready, 1)
                    for t in range(6):
                        m, c = t // 2, t % 2
                        toks = slice(c * HALF, (c + 1) * HALF)
                        dve.wait_ge(op_ready, at(6, b, t + 1))
                        dve.wait_ge(xres_ready, at(3, b, 3))
                        dve.wait_ge(out_dma, at(16, b, 0))
                        dve.scalar_tensor_tensor(out=xa[:, m, toks], in0=pW[:, t % 4, :], scalar=g_col,
                                                 in1=xres[:, m, toks], op0=ALU.mult, op1=ALU.add)\
                           .then_inc(xa_ready, 1)
                else:
                    for kind, i, _ in ITEMS:
                        item(kind, i, b, True)
                        item(kind, i, b, False)

            samples(dve, iteration)

        @block.gpsimd
        def _(pool):
            pool.memset(small[0:1, 32:33], 1.0).then_inc(prep_pool, 1)
            pool.memset(narrow[:, :], 0.0).then_inc(prep_pool, 1)
            pool.memset(stat[:, :, :], 0.0).then_inc(prep_pool, 1)

            def item(kind, n, b):
                a = b - 1
                if kind == "ln_scale":
                    for c in range(2):
                        toks = slice(c * HALF, (c + 1) * HALF)
                        pool.wait_ge(ln_rs, at(4, a, 2 * n + c + 1))
                        pool.tensor_tensor(lnx_of[n][:, :, toks], lnx_of[n][:, :, toks],
                                           prob[:, c * HALF:(c + 1) * HALF].unsqueeze(1).broadcast_to([128, KT, HALF]),
                                           ALU.mult).then_inc(ln_xn, 1)

            def iteration(b, layer0, layer1):
                if layer0:
                    for k in range(KT):
                        pool.wait_ge(loc_ready, at(3, b, k + 1))
                        pool.tensor_tensor(xres[:, k, :], xres[:, k, :], y[:, k, :], ALU.add).then_inc(xres_ready, 1)
                    for d in range(2):
                        for r, n, k in rows(d):
                            for kind, i in SLOTS[r] if layer1 else ():
                                item(kind, i, b)
                            if k == 0:
                                last = r + VK
                                if n:
                                    pool.wait_ge(y_done, at(ROWS, b, r))
                                else:
                                    pool.wait_ge(du_ready, at(6, b, 3 * d + KT))
                                    pool.wait_ge(split_step, at(10, b, 10))
                                    pool.wait_ge(y_done, at(ROWS, b, r))
                                pool.wait_ge(bsb_ready, at(2 * NS, b, NS * d + n + 1))
                                pool.tensor_tensor(hb[last % 3][:, :], du[d][:, VK, :], b_sb[:, :], ALU.mult)\
                                    .then_inc(m1p_done, 1)
                            pool.wait_ge(m2_done, at(ROWS, b, r + 1))
                            if r < KT:
                                pool.wait_ge(yd_ready, at(6, b, 6))
                            else:
                                pool.wait_ge(y_done, at(ROWS, b, r - 2))
                            pool.tensor_tensor(y[:, k, :], y[:, k, :], hb[r % 3][:, :], ALU.add).then_inc(y_done, 1)
                else:
                    for kind, i, _ in ITEMS:
                        item(kind, i, b)

            samples(pool, iteration)


def constants():
    import numpy as np

    c = np.zeros((128, 512), np.float32)
    c[:, 0:128] = np.eye(128)
    c[:, 128:256] = 1.0 / C
    c[:, 256:384] = np.triu(np.full((128, 128), -1e30), 1)
    c[0:96, 384:416] = np.tile(np.eye(32), (3, 1))
    k32 = np.zeros((KI, 2 * C), np.float32)
    ch = np.arange(C)
    member = (ch[:, None] // 12 == np.arange(KI)[None, :]).astype(np.float32)
    k32[:, 0:C] = member.T
    k32[0:12, C:] = (ch[None, :] % 12 == np.arange(12)[:, None])
    c = np.concatenate([c[:, 0:416], member.reshape(KT, 128, KI).transpose(1, 0, 2).reshape(128, KT * KI)], 1)
    return c, k32


def kernel(**inputs):
    import concourse.bacc as bacc
    import numpy as np
    from concourse.bass_utils import run_bass_kernel_spmd

    i0 = {n[8:]: np.asarray(v) for n, v in inputs.items() if n.startswith("L0_conv_")}
    at = {n[8:]: np.asarray(v) for n, v in inputs.items() if n.startswith("L1_attn_")}
    ff = {n[7:]: np.asarray(v) for n, v in inputs.items() if n.startswith("L1_ffn_")}
    k128, k32 = constants()
    xp = i0["x_proj_w"]
    arrays = {
        "x": np.asarray(inputs["x"]).reshape(NB, C, L),
        "chan": np.concatenate([
            np.stack([i0["norm_w"], i0["conv1d_b"], i0["dt_proj_b"], i0["D_param"], i0["dw_b"],
                      at["bq"], at["bk"], at["bv"], at["bo"]], 1),
            i0["conv1d_w"], i0["dw_w"].reshape(C, 9), i0["A_log"]], 1),
        "scal": np.stack([i0["scale_mod"], i0["res_scale"]], 1),
        "k128": k128,
        "k32": k32,
        "w_in": i0["in_proj_w"].T,
        "w_x": np.concatenate([xp[RANK:], xp[:RANK]], 0).T,
        "w_dt": i0["dt_proj_w"].T,
        "w_out": i0["out_proj_w"].T,
        "wq": at["Wq"], "wk": at["Wk"], "wv": at["Wv"], "wo": at["Wo"],
        "fc1": ff["c_fc_1"].T, "fc2": ff["c_fc_2"].T, "pr1": ff["c_proj_1"].T, "pr2": ff["c_proj_2"],
    }
    nc = bacc.Bacc("TRN2", target_bir_lowering=False, num_devices=1)
    feed, args = {}, []
    for name, a in arrays.items():
        a = np.ascontiguousarray(a)
        feed[f"in_{name}"] = a
        args.append(nc.dram_tensor(f"in_{name}", a.shape, mybir.dt.from_np(a.dtype), kind="ExternalInput").ap())
    out = nc.dram_tensor("out_x", (NB, C, L), F32, kind="ExternalOutput").ap()
    hybrid_block(nc, *args, out)
    r = run_bass_kernel_spmd(nc, [feed], core_ids=[0])
    return r.results[0]["out_x"].reshape(NB, C, HH, WW)
```

```python
from contextlib import ExitStack

import concourse.bass as bass
from concourse import mybir

F32 = mybir.dt.float32
BF16 = mybir.dt.bfloat16
ALU = mybir.AluOpType
ACT = mybir.ActivationFunctionType
AX = mybir.AxisListType.X

NB, C, HH, WW = 8, 384, 32, 32
L = HH * WW
KT = C // 128
HALF = L // 2
NS = 16
NTAP = 4
RANK = 24
NH, DH = 6, 64
QT = L // 128
FF = 1536
NF = FF // 128
KI = 32
WP = WW + 2
UP = L + 2 * (NTAP - 1)
ROWS = 2 * NS * KT
DROWS = NS * KT
VK = KT - 1
VROWS = 2 * NS * VK

(V_NW, V_CB, V_DTB, V_D, V_DWB, V_BQ, V_BK, V_BV, V_BO) = range(9)
V_CW, V_DW, V_A = 9, 13, 22
NV = V_A + NS

GROUPS = []
for _h in range(0, NH, 2):
    for _g in (_h, _h + 1):
        GROUPS += [[(_g, QT - 1, 0)]] + [[(_g, i, 0), (_g, QT - 2 - i, 128 * (i + 1))] for i in range(QT // 2 - 1)]
    GROUPS.append([(_h, QT // 2 - 1, 0), (_h + 1, QT // 2 - 1, HALF)])
NG = len(GROUPS)

NPJ = 20
FGRP = 3
NFG = NF // FGRP
ITEMS = (
    [("step_bc", 0, 0.5)] + [("step_in", k, 0.5) for k in range(KT)]
    + [("step_log", 0, 1.0)] + [("step_sum", k, 0.4) for k in range(KT)]
    + [("ln_mean", 0, 0.8), ("ln_var", 0, 0.9), ("ln_scale", 0, 0.765)]
    + [("proj", t, 0.75) for t in range(NPJ)]
    + [x for p in range(NG + 1) for x in (("scores", p, 0.9), ("values", p, 0.9))]
    + [("ctx_t", g, 0.4) for g in range(6)]
    + [("wo", t, 0.75) for t in range(6)]
    + [("ln_mean", 1, 0.8), ("ln_var", 1, 0.9), ("ln_scale", 1, 0.9), ("mlp_in", 0, 1.395)]
    + [x for c in range(2) for x in [("mlp", c * (NFG + 1) + q, 1.6) for q in range(NFG + 1)]
       + [("mlp_out", c, 0.7)]]
    + [("next_square", 0, 0.8), ("next_mean", 0, 1.0), ("next_norm", 0, 1.0)]
)


def slots():
    total = sum(w for _, _, w in ITEMS)
    out, at = [[] for _ in range(ROWS)], 0.0
    for kind, n, w in ITEMS:
        out[min(ROWS - 1, int(at * ROWS / total))].append((kind, n))
        at += w
    return out


SLOTS = slots()
NEXT = ("next_square", "next_mean", "next_norm")
CROWDED = [n for n in range(1, NG + 1) if any({("values", n - 1), ("scores", n)} <= set(row) for row in SLOTS)]
STEP = ("step_bc", "step_in", "step_log", "step_sum")
ALONE = [(kind, n) for kind, n, _ in ITEMS if kind not in NEXT + STEP]


def beside(r, layer1, more):
    return [(kind, n) for kind, n in SLOTS[r] if kind in STEP or layer1 and (more or kind not in NEXT)]


def hybrid_block(nc, x, chan, scal, k128, k32, w_in, w_x, w_dt, w_out, wq, wk, wv, wo, fc1, fc2, pr1, pr2, kept, out):
    with ExitStack() as ctx:
        def sb(name, shape, dt=F32):
            return ctx.enter_context(nc.sbuf_tensor(name, shape, dt))

        def sem(name):
            return ctx.enter_context(nc.semaphore(name))

        vec = sb("vec", [128, KT, NV])
        consts = sb("consts", [128, 256])
        ident, ones_c = consts[:, 0:128], consts[:, 128:256]
        sel_bf = sb("sel_bf", [128, 32], BF16)
        ident_bf = sb("ident_bf", [128, 128], BF16)
        causal_bf = sb("causal_bf", [128, 128], BF16)
        tiny = sb("tiny", [128, 8])
        rs_col, g_col, eps6, eps5, bq_s = tiny[:, 0:1], tiny[:, 1:2], tiny[:, 2:3], tiny[:, 3:4], tiny[:, 4:7]
        xp_w = sb("xp_w", [128, KT, 56])
        op_w = sb("op_w", [128, KT, C])
        q_w, k_w, v_w, o_w = (sb(n, [128, KT, C]) for n in ("q_w", "k_w", "v_w", "o_w"))
        fc_bf = sb("fc_bf", [128, FF], BF16)
        mixed = sb("mixed", [128, C])
        dt_w = [mixed[32:32 + RANK, 0:C], mixed[96:96 + RANK, 0:C]]
        kout_w = mixed[64:64 + KI, 0:C]
        pr_w = sb("pr_w", [128, NF, KI])
        kin_w = sb("kin_w", [128, KT, 4 * KI])
        small = sb("small", [128, 64])
        stat = sb("stat", [128, 3, 4])

        xres = sb("xres", [128, KT, L])
        delta = [sb("delta", [128, KT, L]), xres]
        du_f = sb("du_f", [128, KT, L])
        uc_b = sb("uc_b", [128, KT, L])
        y = sb("y", [128, KT, L])
        zs = sb("zs", [128, KT, L])
        dA = [sb(f"dA{i}", [128, L]) for i in range(2)]
        hb = [sb(f"hb{i}", [128, L]) for i in range(3)]
        b_sb = sb("b_sb", [128, L])
        bc3 = [sb(f"bc3_{d}", [96, L], BF16) for d in range(2)]
        narrow = sb("narrow", [128, L])
        dtr = [narrow[32:32 + RANK, :], narrow[96:96 + RANK, :]]
        rr = narrow[64:64 + KI, :]

        fc_raw, fc_part = (t[:, 0:2, :].rearrange("p k t -> p (k t)")[:, 0:FF] for t in (zs, y))
        early = du_f[:, 0, 0:256]

        xa = sb("xa", [128, KT, L])
        xn_area = sb("xn_area", [128, KT * L])
        area0 = sb("area0", [128, KT * HH * WP + KT * 2 * WP])
        area1 = sb("area1", [128, KT * UP])
        area2 = sb("area2", [128, KT * L])
        prob = sb("prob", [128, L])
        pt = sb("pt", [128, L])

        xr_a, xr_b, xr_rest = pt[:, 0:HALF].bitcast(BF16), pt[:, HALF:L].bitcast(BF16), prob

        def tiled(area):
            return area[:, 0:KT * L].rearrange("p (k t) -> p k t", k=KT)

        ip_w = xn_area[:, 0:KT * 2 * C].rearrange("p (k e) -> p k e", k=KT)
        xnp = area0[:, :].rearrange("p (k h w) -> p k h w", k=KT, h=HH + 2)
        up = area1[:, :].rearrange("p (k t) -> p k t", k=KT)
        uc_f = tiled(area2)
        xnext, xsq, rstd = tiled(area2), tiled(area1), prob
        gate = du_f
        soft = [[dA[0], dA[1], b_sb], [tiled(area1)[:, k, :] for k in range(KT)]]
        uc = [uc_f, uc_b]
        du = [du_f, uc_b]
        xn1, xn2 = tiled(xn_area), tiled(area1)
        sq_of = [tiled(area0), tiled(area2)]
        lnx_of = [xn1, xn2]
        qT, kT, ctxT = tiled(area0), tiled(area1), tiled(area0)
        vtok = area2[:, :].rearrange("p (j c) -> p j c", j=QT)
        ctxk = xn_area[:, :].rearrange("p (j c) -> p j c", j=QT)
        hid = area0[:, 0:2 * FGRP * HALF].rearrange("p (s f t) -> p s f t", s=2, f=FGRP)

        pBC = [ctx.enter_context(nc.psum_tensor(f"pBC{i}", [128, L], F32)) for i in range(2)]
        pW = ctx.enter_context(nc.psum_tensor("pW", [128, 4, HALF], F32))
        bc_raw = [pt[64 * d:64 * d + 32, :] for d in range(2)]
        pS = pW[:, 0:2, :].rearrange("p b t -> p (b t)")
        pT = pW[:, 2:4, :].rearrange("p b t -> p (b t)")
        dt_bank = [pBC[0], pBC[1], pS, pT, pS, pT]

        consts_in, prep_act, prep_dve, prep_pe, prep_pool, fc_split = (
            sem(n) for n in ("consts_in", "prep_act", "prep_dve", "prep_pe", "prep_pool", "fc_split"))
        x_in, xn_in, win_in, out_dma, kept_out, kept_in = (
            sem(n) for n in ("x_in", "xn_in", "win_in", "out_dma", "kept_out", "kept_in"))
        pad_zero, sq_ready, ms_ready, ms_log, rstd_ready, xn_ready, ip_ready, ip_evac = (
            sem(n) for n in ("pad_zero", "sq_ready", "ms_ready", "ms_log", "rstd_ready", "xn_ready", "ip_ready",
                             "ip_evac"))
        dw_step, dwt_ready, dwp_step, sig_ready, loc_ready, xres_ready, cv_step, uc_ready = (
            sem(n) for n in ("dw_step", "dwt_ready", "dwp_step", "sig_ready", "loc_ready", "xres_ready",
                             "cv_step", "uc_ready"))
        xd_ready, xd_evac, split_step, yd_ready = (sem(n) for n in ("xd_ready", "xd_evac", "split_step", "yd_ready"))
        dt_ready, relu_done, sp_abs, sp_exp, sp_ready, delta_ready, du_ready = (
            sem(n) for n in ("dt_ready", "relu_done", "sp_abs", "sp_exp", "sp_ready", "delta_ready", "du_ready"))
        b_ready, c_ready, bsb_ready, da_ready, m1_done, m1p_done, scan_done, m2_done, y_done = (
            sem(n) for n in ("b_ready", "c_ready", "bsb_ready", "da_ready", "m1_done", "m1p_done", "scan_done",
                             "m2_done", "y_done"))
        yz_ready, op_ready, xa_ready = (sem(n) for n in ("yz_ready", "op_ready", "xa_ready"))
        ln_mean, ln_xc, ln_sq, ln_var, ln_log, ln_rs, ln_xn, ln_xp = (
            sem(n) for n in ("ln_mean", "ln_xc", "ln_sq", "ln_var", "ln_log", "ln_rs", "ln_xn", "ln_xp"))
        pj_ready, pj_evac, s_ready, nmax_ready, p_ready, tr_ready, pt_ready, pv_done, rinv_ready, ctx_ready = (
            sem(n) for n in ("pj_ready", "pj_evac", "s_ready", "nmax_ready", "p_ready", "tr_ready", "pt_ready",
                             "pv_done", "rinv_ready", "ctx_ready"))
        ct_ready, ct_evac, wo_ready, wo_add = (sem(n) for n in ("ct_ready", "ct_evac", "wo_ready", "wo_add"))
        xr_ready, xr_step, fc_ready, h_ready, r_done, r_evac, fo_ready, x2_ready = (
            sem(n) for n in ("xr_ready", "xr_step", "fc_ready", "h_ready", "r_done", "r_evac", "fo_ready",
                             "x2_ready"))

        def at(per, b, n):
            v = b * per + n
            return max(v, 0) if isinstance(v, int) else v

        def alone(b):
            return isinstance(b, int) and b == NB

        def scores_bank(b, n):
            return pBC[0] if alone(b) and n % 2 else pS

        def prob_bank(b, half):
            return pBC[1][:, half * HALF:(half + 1) * HALF] if alone(b) else pW[:, 2 + half, :]

        def latest(b):
            return min(b, NB - 1) if isinstance(b, int) else b

        def samples(eng, iteration):
            iteration(0, True, False, True)
            with eng.Fori(1, NB - 1) as b:
                iteration(b, True, True, True)
            iteration(NB - 1, True, True, False)
            iteration(NB, False, True, False)

        def rows():
            return [(r, r // DROWS, r % DROWS // KT, r % KT) for r in range(ROWS)]

        def flow(d, ap):
            return ap if d == 0 else ap[:, ::-1]

        block = ctx.enter_context(nc.Block())

        @block.sync
        def _(sp):
            def load_next(b):
                sp.dma_start(xnext, x[b].rearrange("(k p) t -> p k t", p=128)).then_inc(xn_in, 16)

            sp.dma_start(ip_w, w_in.rearrange("(k p) e -> p k e", p=128)).then_inc(win_in, 16)
            load_next(0)
            for dst, src in ((vec[:, :, :], chan.rearrange("(k p) v -> p k v", p=128)),
                             (consts[:, :], k128[:, 0:256]), (early[:, :], k128[:, 256:512]),
                             (small[0:1, 0:2], scal[:, :]),
                             (prob[0:KI, 0:2 * C], k32[:, :]),
                             (small[0:12, 2:3], fc2[:, :]),
                             (small[0:12, 3:4], pr2[:, :]),
                             (xp_w[:, :, :], w_x.rearrange("(k p) e -> p k e", p=128)),
                             (dt_w[0], w_dt[:, :]), (dt_w[1], w_dt[:, :]),
                             (op_w[:, :, :], w_out.rearrange("(k p) e -> p k e", p=128)),
                             (q_w[:, :, :], wq.rearrange("(k p) e -> p k e", p=128)),
                             (k_w[:, :, :], wk.rearrange("(k p) e -> p k e", p=128)),
                             (v_w[:, :, :], wv.rearrange("(k p) e -> p k e", p=128)),
                             (o_w[:, :, :], wo.rearrange("(k p) e -> p k e", p=128)),
                             (fc_raw[0:KI, :], fc1[:, :]), (fc_raw[KI:2 * KI, :], fc1[:, :]),
                             (fc_raw[2 * KI:3 * KI, :], fc1[:, :]), (fc_raw[3 * KI:4 * KI, :], fc1[:, :]),
                             (pr_w[:, :, :], pr1.rearrange("(f p) i -> p f i", p=128))):
                sp.dma_start(dst, src).then_inc(consts_in, 16)

            def iteration(b, layer0, layer1, more):
                if layer0:
                    sp.wait_ge(xa_ready, at(6, b, 0))
                    sp.dma_start(xres[:, :, :], x[b].rearrange("(k p) t -> p k t", p=128)).then_inc(x_in, 16)
                    sp.wait_ge(xres_ready, at(3, b, 3))
                    sp.dma_start(kept.rearrange("(k p) t -> p k t", p=128), xres[:, :, :]).then_inc(kept_out, 16)
                if layer1:
                    if more:
                        sp.wait_ge(ct_evac, at(6, b, 0))
                        sp.dma_start(ip_w, w_in.rearrange("(k p) e -> p k e", p=128)).then_inc(win_in, 16)
                        sp.wait_ge(ln_var, at(4, b, 0))
                        load_next(b + 1)
                    sp.wait_ge(x2_ready, at(2, b, 0))
                    a = b - 1
                    sp.dma_start(out[a].rearrange("(k p) t -> p k t", p=128), xa[:, :, :]).then_inc(out_dma, 16)

                elif more:
                    sp.wait_ge(du_ready, at(6, b, 3))
                    load_next(b + 1)
                if layer0:
                    sp.wait_ge(kept_out, at(16, b, 16))
                    sp.wait_ge(da_ready, at(ROWS, b, ROWS))
                    sp.dma_start(xres[:, :, :], kept.rearrange("(k p) t -> p k t", p=128)).then_inc(kept_in, 16)

            samples(sp, iteration)
            sp.wait_ge(out_dma, 16 * NB)
            sp.wait_ge(win_in, 16 * (NB - 1))
            sp.wait_ge(xn_in, 16 * NB)
            sp.wait_ge(x_in, 16 * NB)
            sp.wait_ge(kept_out, 16 * NB)
            sp.wait_ge(kept_in, 16 * NB)

        NCONST = 20 * 16

        @block.tensor
        def _(pe):
            pe.wait_ge(consts_in, NCONST)
            rep = prob[0:12, C:2 * C]
            for k in range(KT):
                pe.matmul(pW[:, 0, k:k + 1], rep[:, 128 * k:128 * k + 128], small[0:12, 2:3], start=True, stop=True)
            pe.matmul(pW[0:KI, 1, 0:C], small[0:12, 3:4].broadcast_to([12, KI]), rep, start=True, stop=True)
            pe.wait_ge(prep_pool, 1)
            pe.matmul(pW[:, 2, 0:2], small[0:1, 32:33].broadcast_to([1, 128]), small[0:1, 0:2],
                      start=True, stop=True).then_inc(prep_pe, 1)
            pe.wait_ge(prep_dve, 1)

            def project(bank, w, cols, src, toks, done):
                for k in range(KT):
                    mm = pe.matmul(bank, w[:, k, cols], src[:, k, toks], start=(k == 0), stop=(k == KT - 1))
                mm.then_inc(done, 1)

            def in_project(b, part):
                if part == 0:
                    pe.wait_ge(xn_ready, at(3, b, 3))
                    pe.wait_ge(rstd_ready, at(1, b, 1))
                    pe.wait_ge(win_in, 16 if isinstance(b, int) else at(16, b, 0))
                else:
                    pe.wait_ge(xa_ready, at(6, b, 0))
                for t in range(6 * part, 6 * part + 6):
                    m, c = t // 2, t % 2
                    if t % 6 >= 4:
                        pe.wait_ge(ip_evac, at(12, b, t - 3))
                    elif t >= 6:
                        pe.wait_ge(ip_evac, at(12, b, 6))
                    for k in range(KT):
                        mm = pe.matmul(pW[:, t % 4, :], ip_w[:, k, 128 * m:128 * m + 128],
                                       xnp[:, k, 1 + 16 * c:17 + 16 * c, 1:1 + WW],
                                       start=(k == 0), stop=(k == KT - 1))
                    mm.then_inc(ip_ready, 1)

            def average(bank, src, toks, done):
                for k in range(KT):
                    mm = pe.matmul(bank, ones_c, src[:, k, toks], start=(k == 0), stop=(k == KT - 1))
                mm.then_inc(done, 1)

            def step_size(b, d, k):
                g = KT * d + k
                pe.wait_ge(xd_evac, at(4, b, (1, 1, 2, 4, 4, 4)[g]))
                if g < 2:
                    pe.wait_ge(m2_done, at(ROWS, b, 0))
                if g >= 4:
                    pe.wait_ge(relu_done, at(6, b, g - 1))
                    pe.wait_ge(sp_abs, at(6, b, g - 1))
                for c in range(2):
                    mm = pe.matmul(dt_bank[g][:, c * HALF:(c + 1) * HALF], dt_w[d][:, 128 * k:128 * k + 128],
                                   dtr[d][:, c * HALF:(c + 1) * HALF], start=True, stop=True)
                mm.then_inc(dt_ready, 1)

            def spread(b, d, n, bank, row, done):
                for c in range(2):
                    mm = pe.matmul(bank[:, c * HALF:(c + 1) * HALF], sel_bf[0:96, row:row + 1].broadcast_to([96, 128]),
                                   bc3[d][:, c * HALF:(c + 1) * HALF], start=True, stop=True)
                mm.then_inc(done, 1)

            def spread_b(b, d, n):
                if n == 0:
                    pe.wait_ge(split_step, at(10, b, 5 * (d + 1)))
                if d == 0 and n < 2:
                    pe.wait_ge(relu_done, at(6, b, n + 1))
                    pe.wait_ge(sp_abs, at(6, b, n + 1))
                else:
                    pe.wait_ge(m2_done, at(ROWS, b, DROWS * d + KT * (n - 1)))
                spread(b, d, n, pBC[n % 2], n, b_ready)

            def spread_c(b, d, n):
                pe.wait_ge(bsb_ready, at(2 * NS, b, NS * d + n + 1))
                spread(b, d, n, pBC[n % 2], NS + n, c_ready)

            def scores(b, n):
                a, bank = b - 1, scores_bank(b, n)
                pe.wait_ge(pj_evac, at(NPJ, a, NPJ))
                if alone(b):
                    pe.wait_ge(m2_done, at(ROWS, a, ROWS))
                    if n >= 2:
                        pe.wait_ge(p_ready, at(NG, a, n - 1))
                elif n:
                    pe.wait_ge(p_ready, at(NG, a, n))
                for h, i, c0 in GROUPS[n]:
                    p0, end = DH * (h % 2), c0 + 128 * (i + 1)
                    q = qT[p0:p0 + DH, h // 2, 128 * i:128 * i + 128]
                    for lo, hi in ((c0, min(end, HALF)), (max(c0, HALF), end)):
                        if lo < hi:
                            pe.matmul(bank[:, lo:hi], q, kT[p0:p0 + DH, h // 2, lo - c0:hi - c0],
                                      start=True, stop=hi != end)
                    mm = pe.matmul(bank[:, end - 128:end], ident_bf[:, :], causal_bf[:, :], start=False, stop=True)
                mm.then_inc(s_ready, 1)

            def transpose_prob(b, g):
                a = b - 1
                pe.wait_ge(p_ready, at(NG, a, g + 1))
                for half in range(2):
                    if g:
                        pe.wait_ge(pt_ready, at(2 * NG, a, 2 * g - 1 + half))
                    if g and half and not alone(b):
                        pe.wait_ge(ctx_ready, at(NG, a, g))
                    for j in range(4):
                        mm = pe.transpose(prob_bank(b, half)[:, 128 * j:128 * j + 128],
                                          prob[:, half * HALF + 128 * j:half * HALF + 128 * j + 128], ident)
                    mm.then_inc(tr_ready, 1)

            def item(kind, n, b):
                a = b - 1
                if kind == "step_in":
                    step_size(b, 1, n)
                elif kind == "ln_mean":
                    for c in range(2):
                        if n == 0:
                            pe.wait_ge(xa_ready, at(6, a, 6))
                            pe.wait_ge(relu_done, at(6, latest(b), 6))
                            pe.wait_ge(sp_abs, at(6, latest(b), 6))
                        else:
                            pe.wait_ge(wo_add, at(6, a, 6))
                        average(pW[:, 2 * c, :], xa, slice(c * HALF, (c + 1) * HALF), ln_mean)
                elif kind == "ln_var":
                    for c in range(2):
                        pe.wait_ge(ln_sq, at(4, a, 2 * n + c + 1))
                        average(pW[:, 2 * c + 1, :], sq_of[n],
                                slice(c * HALF, (c + 1) * HALF), ln_var)
                elif kind == "proj":
                    pe.wait_ge(ln_xn, at(2, a, 1))
                    pe.wait_ge(ln_xp, at(2, a, 1))
                    if n >= 4:
                        pe.wait_ge(pj_evac, at(NPJ, a, n - 3))
                    bank = pW[:, n % 4, :]
                    if n < 12:
                        m, c = n % 6 // 2, n % 2
                        project(bank, (q_w, k_w)[n // 6], slice(128 * m, 128 * m + 128), xn1,
                                slice(c * HALF, (c + 1) * HALF), pj_ready)
                    else:
                        j = n - 12
                        for k in range(KT):
                            mm = pe.matmul(bank[:, 0:C], xn1[:, k, 128 * j:128 * j + 128], v_w[:, k, :],
                                           start=(k == 0), stop=(k == KT - 1))
                        mm.then_inc(pj_ready, 1)
                elif kind == "scores" and alone(b):
                    if n:
                        transpose_prob(b, n - 1)
                    for m in ((0, 1) if n == 0 else (n + 1,)):
                        if m < NG:
                            scores(b, m)
                elif kind == "scores":
                    if n < NG:
                        scores(b, n)
                    if n:
                        transpose_prob(b, n - 1)
                elif kind == "values":
                    if n:
                        g = n - 1
                        pe.wait_ge(pt_ready, at(2 * NG, a, 2 * g + 2))
                        if alone(b):
                            pe.wait_ge(ctx_ready, at(NG, a, g))
                        for t, (h, i, c0) in enumerate(GROUPS[g]):
                            for j in range(i + 1):
                                mm = pe.matmul(pW[:, 3, DH * t:DH * t + DH], pt[:, c0 + 128 * j:c0 + 128 * j + 128],
                                               vtok[:, j, DH * h:DH * h + DH], start=(j == 0), stop=(j == i))
                        mm.then_inc(pv_done, 1)
                elif kind == "ctx_t":
                    m, c = n // 2, n % 2
                    pe.wait_ge(ctx_ready, at(NG, a, NG))
                    if n >= 4:
                        pe.wait_ge(ct_evac, at(6, a, n - 3))
                    for j in range(4):
                        mm = pe.transpose(pW[:, n % 4, 128 * j:128 * j + 128],
                                          ctxk[:, 4 * c + j, 128 * m:128 * m + 128], ident)
                    mm.then_inc(ct_ready, 1)
                elif kind == "wo":
                    m, c = n // 2, n % 2
                    pe.wait_ge(ct_evac, at(6, a, 6))
                    if n >= 4:
                        pe.wait_ge(wo_add, at(6, a, n - 3))
                    project(pW[:, n % 4, :], o_w, slice(128 * m, 128 * m + 128), ctxT,
                            slice(c * HALF, (c + 1) * HALF), wo_ready)
                elif kind == "mlp_in":
                    pe.wait_ge(ln_xn, at(2, a, 2))
                    pe.wait_ge(ln_xp, at(2, a, 2))
                    for c in range(2):
                        for k in range(KT):
                            mm = pe.matmul(pW[:, c, :], kin_w[:, k, :],
                                           xn2[:, k, c * HALF:(c + 1) * HALF], start=(k == 0), stop=(k == KT - 1))
                        mm.then_inc(xr_ready, 1)
                elif kind == "mlp":
                    c, q = n // (NFG + 1), n % (NFG + 1)
                    g = c * NFG + q
                    toks = slice(c * HALF, (c + 1) * HALF)

                    def hidden():
                        pe.wait_ge(xr_step, at(5, a, 5))
                        if g:
                            pe.wait_ge(h_ready, at(2 * NFG, a, g))
                        if q == 0 and c:
                            pe.wait_ge(x2_ready, at(2, a, c))
                        for f in range(FGRP):
                            ft = FGRP * q + f
                            pe.matmul(pW[:, f, :], fc_bf[:, 128 * ft:128 * ft + 128], xr_a[:, toks],
                                      start=True, stop=False)
                            mm = pe.matmul(pW[:, f, :], fc_bf[0:2 * KI, 128 * ft:128 * ft + 128],
                                           xr_b[0:2 * KI, toks], start=False, stop=True)
                        mm.then_inc(fc_ready, 1)

                    if q < NFG:
                        hidden()
                    if q >= 1:
                        pe.wait_ge(h_ready, at(2 * NFG, a, g))
                        if q == 1 and c:
                            pe.wait_ge(r_evac, at(2, a, c))
                        for f in range(FGRP):
                            ft = FGRP * (q - 1) + f
                            mm = pe.matmul(pW[0:KI, 3, :], pr_w[:, ft, :], hid[:, (g - 1) % 2, f, :],
                                           start=(ft == 0), stop=(ft == NF - 1))
                        mm.then_inc(r_done, 1)
                elif kind == "mlp_out":
                    pe.wait_ge(r_evac, at(2, a, n + 1))
                    for m in range(KT):
                        mm = pe.matmul(pW[:, m, :], kout_w[:, 128 * m:128 * m + 128],
                                       rr[:, n * HALF:(n + 1) * HALF], start=True, stop=True)
                    mm.then_inc(fo_ready, 1)
                elif kind == "next_mean":
                    pe.wait_ge(x2_ready, at(2, b, 0))
                    pe.wait_ge(xd_evac, at(4, b + 1, 0))
                    pe.wait_ge(sq_ready, at(3, b + 1, 3))
                    for c in range(2):
                        average(pW[:, c, :], xsq, slice(c * HALF, (c + 1) * HALF), ms_ready)

            def iteration(b, layer0, layer1, more):
                if layer0:
                    if isinstance(b, int) and b == 0:
                        item("next_mean", 0, -1)
                        in_project(0, 0)
                    in_project(b, 1)
                    pe.wait_ge(ip_evac, at(12, b, 12))
                    for d in range(2):
                        pe.wait_ge(uc_ready, at(6, b, 3 * d + 3))
                        for c in range(2):
                            for k in range(KT):
                                mm = pe.matmul(pW[0:56, 2 * d + c, :], xp_w[:, k, :],
                                               uc[d][:, k, c * HALF:(c + 1) * HALF], start=(k == 0), stop=(k == KT - 1))
                        mm.then_inc(xd_ready, 1)
                        if d == 0:
                            for k in range(KT):
                                step_size(b, 0, k)
                    spread_b(b, 0, 0)
                    for r, d, n, k in rows():
                        if k == 0:
                            spread_c(b, d, n)
                        if k == 1 and r + KT < ROWS:
                            spread_b(b, (r + KT) // DROWS, (n + 1) % NS)
                        for kind, i in beside(r, layer1, more):
                            item(kind, i, b)
                    if more:
                        if not layer1:
                            item("next_mean", 0, b)
                        in_project(b + 1, 0)
                    for t in range(6):
                        m, c = t // 2, t % 2
                        if t == 0:
                            pe.wait_ge(yz_ready, at(3, b, 3))
                            pe.wait_ge(x2_ready, at(2, b, 0))
                            if more:
                                pe.wait_ge(ip_evac, at(12, b + 1, 6))
                        if t >= 4:
                            pe.wait_ge(xa_ready, at(6, b, t - 3))
                        project(pW[:, t % 4, :], op_w, slice(128 * m, 128 * m + 128), y,
                                slice(c * HALF, (c + 1) * HALF), op_ready)
                else:
                    for kind, i in ALONE:
                        item(kind, i, b)

            samples(pe, iteration)

        @block.scalar
        def _(act):
            act.wait_ge(consts_in, NCONST)
            act.wait_ge(prep_pool, 3)
            act.activation(vec[:, :, V_A:V_A + NS], vec[:, :, V_A:V_A + NS], ACT.Exp).then_inc(prep_act, 1)
            act.copy(ident_bf[:, :], ident)
            act.copy(causal_bf[:, :], early[:, 0:128])
            act.copy(sel_bf[:, :], early[:, 128:160]).then_inc(prep_act, 1)
            act.wait_ge(prep_dve, 1)

            def narrow_copies(b, d):
                act.wait_ge(xd_ready, at(2, b, d + 1))
                act.copy(dtr[d], pW[32:56, 2 * d:2 * d + 2, :].rearrange("p b t -> p (b t)")).then_inc(xd_evac, 1)
                act.copy(bc_raw[d], pW[0:32, 2 * d:2 * d + 2, :].rearrange("p b t -> p (b t)")).then_inc(xd_evac, 1)

            def soft_abs(b, d, k):
                if d == 0:
                    act.wait_ge(scan_done, at(ROWS, b, 0))
                    act.wait_ge(m1p_done, at(2 * NS, b, 0))
                    act.wait_ge(delta_ready, at(6, b, 0))
                else:
                    act.wait_ge(cv_step, at(24, b, 24))
                act.wait_ge(dt_ready, at(6, b, 3 * d + k + 1))
                act.activation(soft[d][k][:, :], dt_bank[KT * d + k][:, :], ACT.Abs,
                               bias=vec[:, k, V_DTB:V_DTB + 1]).then_inc(sp_abs, 1)

            def soft_exp(b, d, k):
                act.wait_ge(sp_abs, at(6, b, 3 * d + k + 1))
                act.activation(soft[d][k][:, :], soft[d][k][:, :], ACT.Exp, scale=-1.0).then_inc(sp_exp, 1)

            def soft_log(b, d, k):
                act.wait_ge(sp_exp, at(6, b, 3 * d + k + 1))
                act.activation(soft[d][k][:, :], soft[d][k][:, :], ACT.Ln, bias=1.0).then_inc(sp_ready, 1)

            def decay(b, r):
                d, k = r // DROWS, r % KT
                n = r % DROWS // KT
                act.wait_ge(scan_done, at(ROWS, b, r - 1))
                if r % DROWS < KT:
                    act.wait_ge(delta_ready, at(6, b, 3 * d + k + 1))
                act.activation(dA[r % 2][:, :], delta[d][:, k, :], ACT.Exp,
                               scale=vec[:, k, V_A + n:V_A + n + 1]).then_inc(da_ready, 1)

            def tap(b, j):
                if j == 0:
                    act.wait_ge(xn_ready, at(3, b, 3))
                    act.wait_ge(m1p_done, at(2 * NS, b, 0))
                    act.wait_ge(y_done, at(ROWS, b, 0))
                if j > 2:
                    act.wait_ge(dwp_step, at(8, b, j - 2))
                win = xnp[:, VK, j // 3:j // 3 + HH, j % 3:j % 3 + WW]
                dst = gate[:, VK, :] if j == 0 else hb[j % 2][:, :]
                act.activation(dst.rearrange("p (h w) -> p h w", w=WW), win, ACT.Identity,
                               bias=vec[:, VK, V_DWB:V_DWB + 1] if j == 0 else 0.0,
                               scale=vec[:, VK, V_DW + j:V_DW + j + 1]).then_inc(dwt_ready, 1)

            def copy_u(b):
                for t in range(6):
                    m, c = t // 2, t % 2
                    act.wait_ge(ip_ready, at(12, b, t + 1))
                    act.wait_ge(pad_zero, at(6, b, 6))
                    act.copy(up[:, m, NTAP - 1 + c * HALF:NTAP - 1 + (c + 1) * HALF], pW[:, t % 4, :])\
                        .then_inc(ip_evac, 1)
                    if t >= 3:
                        tap(b, t - 3)

            def copy_b(b, d, n):
                act.wait_ge(b_ready, at(2 * NS, b, NS * d + n + 1))
                act.wait_ge(m1_done, at(VROWS, b, VK * (NS * d + n)))
                act.wait_ge(m1p_done, at(2 * NS, b, NS * d + n))
                if d == 0 and n == 0:
                    act.wait_ge(delta_ready, at(6, b, 3))
                act.copy(b_sb[:, :], pBC[n % 2][:, :]).then_inc(bsb_ready, 1)

            def item(kind, n, b, early):
                a = b - 1
                if kind == "step_bc" and early:
                    narrow_copies(b, 1)
                elif kind == "step_in" and not early:
                    soft_abs(b, 1, n)
                    soft_exp(b, 1, n)
                    act.wait_ge(kept_out, at(16, b, 16))
                    act.activation(delta[1][:, n, :], dt_bank[KT + n][:, :], ACT.Relu,
                                   bias=vec[:, n, V_DTB:V_DTB + 1]).then_inc(relu_done, 1)
                elif kind == "step_log" and not early:
                    for k in range(KT):
                        soft_log(b, 1, k)
                elif kind == "ln_var" and early:
                    for c in range(2):
                        if n == 0:
                            act.wait_ge(du_ready, at(6, latest(b), 3))
                        act.wait_ge(ln_xc, at(4, a, 2 * n + c + 1))
                        toks = slice(c * HALF, (c + 1) * HALF)
                        act.activation(sq_of[n][:, :, toks], lnx_of[n][:, :, toks], ACT.Square).then_inc(ln_sq, 1)
                elif kind == "ln_scale" and early:
                    if n == 0:
                        act.wait_ge(split_step, at(10, latest(b), 10))
                    for c in range(2):
                        act.wait_ge(ln_var, at(4, a, 2 * n + c + 1))
                        act.activation(prob[:, c * HALF:(c + 1) * HALF], pW[:, 2 * c + 1, :], ACT.Ln,
                                       bias=eps5).then_inc(ln_log, 1)
                    for c in range(2):
                        act.wait_ge(ln_log, at(4, a, 2 * n + c + 1))
                        act.activation(prob[:, c * HALF:(c + 1) * HALF], prob[:, c * HALF:(c + 1) * HALF], ACT.Exp,
                                       scale=-0.5).then_inc(ln_rs, 1)
                elif kind == "proj" and not early:
                    act.wait_ge(pj_ready, at(NPJ, a, n + 1))
                    act.wait_ge(ln_var, at(4, a, 2))
                    bank = pW[:, n % 4, :]
                    if n < 12:
                        m, c = n % 6 // 2, n % 2
                        toks = slice(c * HALF, (c + 1) * HALF)
                        if n >= 6:
                            act.wait_ge(delta_ready, at(6, latest(b), 6))
                        if n < 6:
                            ev = act.activation(qT[:, m, toks], bank, ACT.Identity, bias=bq_s[:, m:m + 1], scale=0.125)
                        else:
                            ev = act.activation(kT[:, m, toks], bank, ACT.Identity, bias=vec[:, m, V_BK:V_BK + 1])
                    else:
                        ev = act.copy(vtok[:, n - 12, :], bank[:, 0:C])
                    ev.then_inc(pj_evac, 1)
                elif kind == "values" and early:
                    if n:
                        g = n - 1
                        for half in range(2):
                            act.wait_ge(tr_ready, at(2 * NG, a, 2 * g + half + 1))
                            if g:
                                act.wait_ge(pv_done, at(NG, a, g))
                            act.copy(pt[:, half * HALF:(half + 1) * HALF], prob_bank(b, half)).then_inc(pt_ready, 1)
                    if n < NG:
                        act.wait_ge(nmax_ready, at(NG, a, n + 1))
                        if n:
                            act.wait_ge(tr_ready, at(2 * NG, a, 2 * n))
                        else:
                            act.wait_ge(ln_xn, at(2, a, 1))
                            act.wait_ge(ln_xp, at(2, a, 1))
                        if n >= 2:
                            act.wait_ge(ctx_ready, at(NG, a, n - 1))
                        for t, (h, i, c0) in enumerate(GROUPS[n]):
                            st = 2 * (n % 2) + t
                            end = c0 + 128 * (i + 1)
                            ex = act.activation(prob[:, c0:end], scores_bank(b, n)[:, c0:end], ACT.Exp,
                                                bias=stat[:, 0, st:st + 1], accum_out=stat[:, 1, st:st + 1])
                        ex.then_inc(p_ready, 1)
                elif kind == "ctx_t" and not early:
                    m, c = n // 2, n % 2
                    act.wait_ge(ct_ready, at(6, a, n + 1))
                    act.activation(ctxT[:, m, c * HALF:(c + 1) * HALF], pW[:, n % 4, :], ACT.Identity,
                                   bias=vec[:, m, V_BV:V_BV + 1]).then_inc(ct_evac, 1)
                elif kind == "mlp_in" and not early:
                    act.wait_ge(xr_ready, at(2, a, 2))
                    act.wait_ge(pv_done, at(NG, a, NG))
                    act.copy(xr_a, pS).then_inc(xr_step, 1)
                elif kind == "mlp" and not early:
                    c, q = n // (NFG + 1), n % (NFG + 1)
                    g = c * NFG + q
                    if q < NFG:
                        act.wait_ge(fc_ready, at(2 * NFG, a, g + 1))
                        if g >= 2:
                            act.wait_ge(r_done, at(2 * NFG, a, g - 1))
                        act.activation(hid[:, g % 2, :, :], pW[:, 0:FGRP, :], ACT.Gelu).then_inc(h_ready, 1)
                    else:
                        act.wait_ge(r_done, at(2 * NFG, a, g))
                        act.copy(rr[:, c * HALF:(c + 1) * HALF], pW[0:KI, 3, :]).then_inc(r_evac, 1)
                elif kind == "next_square" and early:
                    act.wait_ge(xn_in, at(16, b + 1, 16))
                    act.wait_ge(xr_ready, at(2, b, 0))
                    act.wait_ge(cv_step, at(24, b + 1, 0))
                    for k in range(KT):
                        act.activation(xsq[:, k, :], xnext[:, k, :], ACT.Square).then_inc(sq_ready, 1)
                elif kind == "next_mean" and not early:
                    act.wait_ge(ms_ready, at(2, b + 1, 2))
                    act.wait_ge(tr_ready, at(2 * NG, b, 0))
                    act.activation(rstd[:, :], pS, ACT.Ln, bias=eps6).then_inc(ms_log, 1)
                    act.wait_ge(ms_log, at(1, b + 1, 1))
                    act.activation(rstd[:, :], rstd[:, :], ACT.Exp, scale=-0.5).then_inc(rstd_ready, 1)

            def iteration(b, layer0, layer1, more):
                if layer0:
                    if isinstance(b, int) and b == 0:
                        item("next_square", 0, -1, True)
                        item("next_mean", 0, -1, False)
                        copy_u(0)
                    for t in range(6, 12):
                        m, c = t // 2 - 3, t % 2
                        act.wait_ge(ip_ready, at(12, b, t + 1))
                        act.wait_ge(yz_ready, at(3, b, 0))
                        act.activation(zs[:, m, c * HALF:(c + 1) * HALF], pW[:, t % 4, :], ACT.Silu)\
                            .then_inc(ip_evac, 1)
                        tap(b, t - 3)
                    for d in range(2):
                        for k in range(KT):
                            act.wait_ge(cv_step, at(24, b, 12 * d + 9 + k + 1))
                            act.activation(uc[d][:, k, :], uc[d][:, k, :], ACT.Silu,
                                           bias=vec[:, k, V_CB:V_CB + 1]).then_inc(uc_ready, 1)
                    narrow_copies(b, 0)
                    for k in range(KT):
                        if k < VK:
                            act.wait_ge(dw_step, at(9 * VK, b, 8 * VK + k + 1))
                        else:
                            act.wait_ge(dwp_step, at(8, b, 8))
                        act.activation(gate[:, k, :], gate[:, k, :], ACT.Sigmoid).then_inc(sig_ready, 1)
                    for k in range(KT):
                        soft_abs(b, 0, k)
                    for k in range(KT):
                        soft_exp(b, 0, k)
                    for k in range(KT):
                        soft_log(b, 0, k)
                    decay(b, 0)
                    copy_b(b, 0, 0)
                    for r, d, n, k in rows():
                        for kind, i in beside(r, layer1, more):
                            item(kind, i, b, True)
                        if r + 1 < ROWS:
                            decay(b, r + 1)
                        if k == 2 and r + 1 < ROWS:
                            copy_b(b, (r + 1) // DROWS, (n + 1) % NS)
                        for kind, i in beside(r, layer1, more):
                            item(kind, i, b, False)
                    if more:
                        if not layer1:
                            item("next_square", 0, b, True)
                            item("next_mean", 0, b, False)
                        copy_u(b + 1)
                else:
                    for kind, i in ALONE:
                        item(kind, i, b, True)
                        item(kind, i, b, False)

            samples(act, iteration)

        @block.vector
        def _(dve):
            dve.memset(eps6, 1e-6)
            dve.memset(eps5, 1e-5)
            dve.wait_ge(prep_act, 2)
            dve.tensor_copy(fc_bf[:, :], fc_raw).then_inc(fc_split, 1)
            dve.wait_ge(fc_split, 1)
            dve.tensor_tensor(fc_raw, fc_raw, fc_bf[:, :], ALU.subtract).then_inc(fc_split, 1)
            dve.wait_ge(fc_split, 2)
            dve.tensor_copy(fc_bf[KI:2 * KI, :], fc_raw[KI:2 * KI, :])
            dve.tensor_copy(fc_bf[2 * KI:3 * KI, :], fc_raw[2 * KI:3 * KI, :]).then_inc(fc_split, 1)
            dve.wait_ge(fc_split, 3)
            dve.tensor_tensor(fc_part[2 * KI:3 * KI, :], fc_raw[2 * KI:3 * KI, :], fc_bf[2 * KI:3 * KI, :],
                              ALU.subtract).then_inc(fc_split, 1)
            dve.wait_ge(fc_split, 4)
            dve.tensor_copy(fc_bf[2 * KI:3 * KI, :], fc_part[2 * KI:3 * KI, :]).then_inc(fc_split, 1)
            dve.tensor_scalar(vec[:, :, V_A:V_A + NS], vec[:, :, V_A:V_A + NS], -1.0, None, ALU.mult)
            dve.tensor_scalar(bq_s, vec[:, :, V_BQ], 0.125, None, ALU.mult)
            dve.wait_ge(prep_pe, 1)
            for k in range(KT):
                dve.tensor_scalar(kin_w[:, k, :].rearrange("p (q i) -> p q i", q=4),
                                  early[:, 160 + KI * k:192 + KI * k].unsqueeze(1).broadcast_to([128, 4, KI]),
                                  pW[:, 0, k:k + 1], None, ALU.mult)
            dve.tensor_tensor(kout_w, prob[0:KI, 0:C], pW[0:KI, 1, 0:C], ALU.mult)
            dve.tensor_copy(small[:, 8:10], pW[:, 2, 0:2]).then_inc(prep_dve, 1)
            dve.wait_ge(prep_dve, 1)
            dve.tensor_copy(rs_col, small[:, 9:10])
            dve.tensor_tensor(g_col, small[:, 8:9], small[:, 9:10], ALU.mult).then_inc(prep_dve, 1)
            dve.wait_ge(prep_dve, 2)

            def relu(b, k):
                dve.wait_ge(sp_abs, at(6, b, k + 1))
                dve.wait_ge(da_ready, at(ROWS, b, 0))
                dve.tensor_scalar(delta[0][:, k, :], dt_bank[k][:, :], vec[:, k, V_DTB:V_DTB + 1], 0.0,
                                  ALU.add, ALU.max).then_inc(relu_done, 1)

            def soft_sum(b, d, k):
                dve.wait_ge(relu_done, at(6, b, 3 * d + k + 1))
                dve.wait_ge(sp_ready, at(6, b, 3 * d + k + 1))
                dve.tensor_tensor(delta[d][:, k, :], delta[d][:, k, :], soft[d][k][:, :], ALU.add)\
                   .then_inc(delta_ready, 1)

            def times_u(b, d, k):
                dve.wait_ge(delta_ready, at(6, b, 3 * d + k + 1))
                if d == 0:
                    dve.wait_ge(m1_done, at(VROWS, b, 0))
                    dve.wait_ge(m1p_done, at(2 * NS, b, 0))
                    dve.wait_ge(xres_ready, at(3, b, 3))
                else:
                    dve.wait_ge(yd_ready, at(6, b, 6))
                dve.tensor_tensor(du[d][:, k, :], delta[d][:, k, :], uc[d][:, k, :], ALU.mult).then_inc(du_ready, 1)

            def depthwise(b, lo, hi):
                for step in range(lo, hi):
                    j, k = step // VK, step % VK
                    win = xnp[:, k, j // 3:j // 3 + HH, j % 3:j % 3 + WW]
                    acc = gate[:, k, :].rearrange("p (h w) -> p h w", w=WW)
                    w = vec[:, k, V_DW + j:V_DW + j + 1]
                    if j == 0:
                        dve.wait_ge(xn_ready, at(3, b, k + 1))
                        dve.tensor_scalar(acc, win, w, vec[:, k, V_DWB:V_DWB + 1], ALU.mult, ALU.add)\
                           .then_inc(dw_step, 1)
                    else:
                        dve.wait_ge(dw_step, at(9 * VK, b, step - VK + 1))
                        dve.scalar_tensor_tensor(out=acc, in0=win, scalar=w, in1=acc, op0=ALU.mult,
                                                 op1=ALU.add).then_inc(dw_step, 1)

            def finish(b, t):
                m, c = t // 2, t % 2
                toks = slice(c * HALF, (c + 1) * HALF)
                dve.wait_ge(op_ready, at(6, b, t + 1))
                dve.wait_ge(kept_in, at(16, b, 16))
                dve.wait_ge(out_dma, at(16, b, 0))
                dve.scalar_tensor_tensor(out=xa[:, m, toks], in0=pW[:, t % 4, :], scalar=g_col,
                                         in1=xres[:, m, toks], op0=ALU.mult, op1=ALU.add).then_inc(xa_ready, 1)

            def causal(b, lo, hi):
                for step in range(lo, hi):
                    d, j, k = step // 12, step % 12 // KT, step % KT
                    off = j if d == 0 else 2 * (NTAP - 1) - j
                    src, w = up[:, k, off:off + L], vec[:, k, V_CW + j:V_CW + j + 1]
                    if j == 0:
                        dve.wait_ge(ip_evac, at(12, b, 2 * k + 2))
                        dve.wait_ge(xn_ready, at(3, b, 3))
                        dve.wait_ge(m1_done, at(VROWS, b, 0))
                        dve.wait_ge(m1p_done, at(2 * NS, b, 0))
                        dve.tensor_scalar(uc[d][:, k, :], src, w, None, ALU.mult).then_inc(cv_step, 1)
                    else:
                        dve.wait_ge(cv_step, at(24, b, step - 2))
                        dve.scalar_tensor_tensor(out=uc[d][:, k, :], in0=src, scalar=w, in1=uc[d][:, k, :],
                                                 op0=ALU.mult, op1=ALU.add).then_inc(cv_step, 1)

            def split(b, d):
                low = prob[64 * d:64 * d + 32, 0:HALF].bitcast(BF16)
                rest, parts = bc_raw[d], bc3[d]
                dve.wait_ge(xd_evac, at(4, b, 2 * d + 2))
                dve.wait_ge(xn_ready, at(3, b, 3))
                dve.wait_ge(c_ready, at(2 * NS, b, 0))
                dve.tensor_copy(parts[0:32, :], rest).then_inc(split_step, 1)
                dve.wait_ge(split_step, at(10, b, 5 * d + 1))
                dve.tensor_tensor(rest, rest, parts[0:32, :], ALU.subtract).then_inc(split_step, 1)
                dve.wait_ge(split_step, at(10, b, 5 * d + 2))
                dve.tensor_copy(low, rest).then_inc(split_step, 1)
                dve.wait_ge(split_step, at(10, b, 5 * d + 3))
                dve.tensor_tensor(parts[64:96, :], rest, low, ALU.subtract).then_inc(split_step, 1)
                dve.tensor_copy(parts[32:64, :], low).then_inc(split_step, 1)

            def skip(b, d):
                for k in range(KT):
                    dve.wait_ge(uc_ready, at(6, b, 3 * d + k + 1))
                    dcol = vec[:, k, V_D:V_D + 1]
                    if d == 0:
                        dve.wait_ge(op_ready, at(6, b, 0))
                        dve.tensor_scalar(y[:, k, :], uc[0][:, k, :], dcol, None, ALU.mult).then_inc(yd_ready, 1)
                    else:
                        dve.wait_ge(yd_ready, at(6, b, k + 1))
                        dve.scalar_tensor_tensor(out=y[:, k, :], in0=uc[1][:, k, :], scalar=dcol,
                                                 in1=y[:, k, :], op0=ALU.mult, op1=ALU.add).then_inc(yd_ready, 1)

            def input_row(b, r, n, k, d):
                if k == 0:
                    dve.wait_ge(bsb_ready, at(2 * NS, b, NS * d + n + 1))
                dve.wait_ge(y_done, at(ROWS, b, r - 2))
                if n == 0:
                    dve.wait_ge(du_ready, at(6, b, 3 * d + k + 1))
                dve.tensor_tensor(hb[r % 3][:, :], du[d][:, k, :], b_sb[:, :], ALU.mult).then_inc(m1_done, 1)

            def scan_row(b, r, n, k, d):
                dve.wait_ge(da_ready, at(ROWS, b, r + 1))
                if k < VK:
                    dve.wait_ge(m1_done, at(VROWS, b, VK * (NS * d + n) + k + 1))
                else:
                    dve.wait_ge(m1p_done, at(2 * NS, b, NS * d + n + 1))
                buf = hb[r % 3]
                dve.tensor_tensor_scan(flow(d, buf[:, :]), flow(d, dA[r % 2][:, :]), flow(d, buf[:, :]), 0.0,
                                       ALU.mult, ALU.add).then_inc(scan_done, 1)

            def output_row(b, r, n, k, d):
                if k == 0:
                    dve.wait_ge(c_ready, at(2 * NS, b, NS * d + n + 1))
                dve.wait_ge(scan_done, at(ROWS, b, r + 1))
                dve.tensor_tensor(hb[r % 3][:, :], hb[r % 3][:, :], pBC[n % 2][:, :], ALU.mult).then_inc(m2_done, 1)

            def item(kind, n, b, early):
                a = b - 1
                if kind == "step_bc" and not early:
                    split(b, 1)
                elif kind == "step_sum" and not early:
                    soft_sum(b, 1, n)
                    times_u(b, 1, n)
                elif kind == "ln_mean" and not early:
                    for c in range(2):
                        toks = slice(c * HALF, (c + 1) * HALF)
                        if n == 0:
                            dve.wait_ge(ip_ready, at(12, latest(b), 12))
                        dve.wait_ge(ln_mean, at(4, a, 2 * n + c + 1))
                        dve.tensor_tensor(lnx_of[n][:, :, toks], xa[:, :, toks],
                                          pW[:, 2 * c:2 * c + 1, :].broadcast_to([128, KT, HALF]),
                                          ALU.subtract).then_inc(ln_xc, 1)
                elif kind == "ln_scale" and not early:
                    toks = slice(0, HALF)
                    dve.wait_ge(ln_rs, at(4, a, 2 * n + 1))
                    dve.tensor_tensor(lnx_of[n][:, :, toks], lnx_of[n][:, :, toks],
                                      prob[:, toks].unsqueeze(1).broadcast_to([128, KT, HALF]), ALU.mult)\
                       .then_inc(ln_xn, 1)
                elif kind == "values" and early and n < NG:
                    dve.wait_ge(s_ready, at(NG, a, n + 1))
                    if n >= 2:
                        dve.wait_ge(p_ready, at(NG, a, n - 1))
                    for t, (h, i, c0) in enumerate(GROUPS[n]):
                        st = 2 * (n % 2) + t
                        mx = dve.tensor_reduce(stat[:, 0, st:st + 1], scores_bank(b, n)[:, c0:c0 + 128 * (i + 1)],
                                               AX, ALU.max, negate=True)
                    mx.then_inc(nmax_ready, 1)
                elif (kind == "scores" and early == (n not in CROWDED) and n >= 2
                      or kind == "values" and not early and n == NG):
                    g = n - 2 if kind == "scores" else n - 1
                    st, nt = 2 * (g % 2), len(GROUPS[g])
                    dve.wait_ge(p_ready, at(NG, a, g + 1))
                    dve.reciprocal(stat[:, 2, st:st + nt], stat[:, 1, st:st + nt]).then_inc(rinv_ready, 1)
                    dve.wait_ge(rinv_ready, at(NG, a, g + 1))
                    dve.wait_ge(pv_done, at(NG, a, g + 1))
                    for t, (h, i, c0) in enumerate(GROUPS[g]):
                        cx = dve.tensor_scalar(ctxk[:, i, DH * h:DH * h + DH], pW[:, 3, DH * t:DH * t + DH],
                                               stat[:, 2, st + t:st + t + 1], None, ALU.mult)
                    cx.then_inc(ctx_ready, 1)
                elif kind == "wo" and not early:
                    m, c = n // 2, n % 2
                    toks = slice(c * HALF, (c + 1) * HALF)
                    dve.wait_ge(wo_ready, at(6, a, n + 1))
                    dve.scalar_tensor_tensor(out=xa[:, m, toks], in0=pW[:, n % 4, :], scalar=vec[:, m, V_BO:V_BO + 1],
                                             in1=xa[:, m, toks], op0=ALU.add, op1=ALU.add).then_inc(wo_add, 1)
                elif kind == "mlp_in" and not early:
                    dve.wait_ge(xr_step, at(5, a, 1))
                    dve.tensor_tensor(xr_rest[:, :], pS, xr_a, ALU.subtract).then_inc(xr_step, 1)
                    dve.wait_ge(xr_step, at(5, a, 2))
                    dve.tensor_copy(xr_b, xr_rest[:, :]).then_inc(xr_step, 1)
                    dve.wait_ge(xr_step, at(5, a, 3))
                    dve.tensor_copy(xr_a[3 * KI:4 * KI, :], xr_b[3 * KI:4 * KI, :]).then_inc(xr_step, 1)
                    dve.tensor_tensor(xr_b[0:KI, :], xr_rest[0:KI, :], xr_b[0:KI, :], ALU.subtract)\
                       .then_inc(xr_step, 1)
                elif kind == "mlp_out" and not early:
                    toks = slice(n * HALF, (n + 1) * HALF)
                    dve.wait_ge(fo_ready, at(2, a, n + 1))
                    dve.wait_ge(wo_add, at(6, a, 6))
                    dve.tensor_tensor(xa[:, :, toks], xa[:, :, toks], pW[:, 0:3, :], ALU.add).then_inc(x2_ready, 1)
                elif kind == "next_norm" and early:
                    dve.wait_ge(r_done, at(2 * NFG, b, 0))
                    dve.wait_ge(ms_ready, at(2, b + 1, 2))
                    for border in (xnp[:, :, 0, :], xnp[:, :, HH + 1, :], xnp[:, :, 1:1 + HH, 0:1],
                                   xnp[:, :, 1:1 + HH, WW + 1:WP], up[:, :, 0:NTAP - 1], up[:, :, UP - NTAP + 1:UP]):
                        dve.memset(border, 0.0).then_inc(pad_zero, 1)
                    dve.wait_ge(rstd_ready, at(1, b + 1, 1))
                    dve.wait_ge(loc_ready, at(3, b + 1, 0))
                    for k in range(KT):
                        dve.scalar_tensor_tensor(out=xnp[:, k, 1:1 + HH, 1:1 + WW],
                                                 in0=xnext[:, k, :].rearrange("p (h w) -> p h w", w=WW),
                                                 scalar=vec[:, k, V_NW:V_NW + 1],
                                                 in1=rstd[:, :].rearrange("p (h w) -> p h w", w=WW),
                                                 op0=ALU.mult, op1=ALU.mult).then_inc(xn_ready, 1)

            def iteration(b, layer0, layer1, more):
                if layer0:
                    if isinstance(b, int) and b == 0:
                        item("next_norm", 0, -1, True)
                    depthwise(b, 0, 16)
                    for t in range(6):
                        if not (isinstance(b, int) and b == 0):
                            finish(b - 1, t)
                        if t == 0:
                            depthwise(b, 16, 18)
                        else:
                            causal(b, 2 * t - 2, 2 * t)
                    causal(b, 10, 24)
                    skip(b, 0)
                    skip(b, 1)
                    split(b, 0)
                    for k in range(KT):
                        dve.wait_ge(sig_ready, at(3, b, k + 1))
                        acc = gate[:, k, :].rearrange("p (h w) -> p h w", w=WW)
                        dve.scalar_tensor_tensor(out=acc, in0=acc, scalar=rs_col, in1=xnp[:, k, 1:1 + HH, 1:1 + WW],
                                                 op0=ALU.mult, op1=ALU.mult).then_inc(loc_ready, 1)
                    for k in range(KT):
                        relu(b, k)
                    for k in range(KT):
                        soft_sum(b, 0, k)
                        if k:
                            times_u(b, 0, k - 1)
                    times_u(b, 0, KT - 1)
                    before = None
                    for r, d, n, k in rows():
                        for kind, i in beside(r, layer1, more):
                            item(kind, i, b, True)
                        if k < VK:
                            input_row(b, r, n, k, d)
                        if before:
                            output_row(b, *before)
                        scan_row(b, r, n, k, d)
                        before = (r, n, k, d)
                        for kind, i in beside(r, layer1, more):
                            item(kind, i, b, False)
                    output_row(b, *before)
                    if more and not layer1:
                        item("next_norm", 0, b, True)
                    if not more:
                        for t in range(6):
                            finish(b, t)
                else:
                    for kind, i in ALONE:
                        item(kind, i, b, True)
                        item(kind, i, b, False)

            samples(dve, iteration)

        @block.gpsimd
        def _(pool):
            pool.memset(small[0:1, 32:33], 1.0).then_inc(prep_pool, 1)
            pool.memset(narrow[:, :], 0.0).then_inc(prep_pool, 1)
            pool.memset(stat[:, :, :], 0.0).then_inc(prep_pool, 1)

            def item(kind, n, b):
                a = b - 1
                if kind == "ln_scale":
                    toks = slice(HALF, L)
                    pool.wait_ge(ln_rs, at(4, a, 2 * n + 2))
                    pool.tensor_tensor(lnx_of[n][:, :, toks], lnx_of[n][:, :, toks],
                                       prob[:, toks].unsqueeze(1).broadcast_to([128, KT, HALF]), ALU.mult)\
                        .then_inc(ln_xp, 1)

            def iteration(b, layer0, layer1, more):
                if layer0:
                    for j in range(1, 9):
                        pool.wait_ge(dwt_ready, at(9, b, j + 1))
                        pool.wait_ge(dwp_step, at(8, b, j - 1))
                        pool.tensor_tensor(gate[:, VK, :], gate[:, VK, :], hb[j % 2][:, :], ALU.add)\
                            .then_inc(dwp_step, 1)
                    for k in range(KT):
                        pool.wait_ge(loc_ready, at(3, b, k + 1))
                        pool.wait_ge(x_in, at(16, b, 16))
                        pool.tensor_tensor(xres[:, k, :], xres[:, k, :], gate[:, k, :], ALU.add).then_inc(xres_ready, 1)
                    for r, d, n, k in rows():
                        for kind, i in beside(r, layer1, more):
                            item(kind, i, b)
                        if k == 0:
                            last = r + VK
                            if d or n:
                                pool.wait_ge(y_done, at(ROWS, b, r))
                                if n == 0:
                                    pool.wait_ge(du_ready, at(6, b, 6))
                            else:
                                pool.wait_ge(du_ready, at(6, b, KT))
                                pool.wait_ge(y_done, at(ROWS, b, r))
                            pool.wait_ge(bsb_ready, at(2 * NS, b, NS * d + n + 1))
                            pool.tensor_tensor(hb[last % 3][:, :], du[d][:, VK, :], b_sb[:, :], ALU.mult)\
                                .then_inc(m1p_done, 1)
                        pool.wait_ge(m2_done, at(ROWS, b, r + 1))
                        if r < KT:
                            pool.wait_ge(yd_ready, at(6, b, 6))
                        else:
                            pool.wait_ge(y_done, at(ROWS, b, r - 2))
                        pool.tensor_tensor(y[:, k, :], y[:, k, :], hb[r % 3][:, :], ALU.add).then_inc(y_done, 1)
                    for k in range(KT):
                        pool.wait_ge(y_done, at(ROWS, b, ROWS))
                        pool.wait_ge(ip_evac, at(12, b, 12))
                        pool.tensor_tensor(y[:, k, :], y[:, k, :], zs[:, k, :], ALU.mult).then_inc(yz_ready, 1)
                else:
                    for kind, i in ALONE:
                        item(kind, i, b)

            samples(pool, iteration)


def constants():
    import numpy as np

    c = np.zeros((128, 512), np.float32)
    c[:, 0:128] = np.eye(128)
    c[:, 128:256] = 1.0 / C
    c[:, 256:384] = np.triu(np.full((128, 128), -1e30), 1)
    c[0:96, 384:416] = np.tile(np.eye(32), (3, 1))
    k32 = np.zeros((KI, 2 * C), np.float32)
    ch = np.arange(C)
    member = (ch[:, None] // 12 == np.arange(KI)[None, :]).astype(np.float32)
    k32[:, 0:C] = member.T
    k32[0:12, C:] = (ch[None, :] % 12 == np.arange(12)[:, None])
    c = np.concatenate([c[:, 0:416], member.reshape(KT, 128, KI).transpose(1, 0, 2).reshape(128, KT * KI)], 1)
    return c, k32


def kernel(**inputs):
    import concourse.bacc as bacc
    import numpy as np
    from concourse.bass_utils import run_bass_kernel_spmd

    i0 = {n[8:]: np.asarray(v) for n, v in inputs.items() if n.startswith("L0_conv_")}
    at = {n[8:]: np.asarray(v) for n, v in inputs.items() if n.startswith("L1_attn_")}
    ff = {n[7:]: np.asarray(v) for n, v in inputs.items() if n.startswith("L1_ffn_")}
    k128, k32 = constants()
    xp = i0["x_proj_w"]
    arrays = {
        "x": np.asarray(inputs["x"]).reshape(NB, C, L),
        "chan": np.concatenate([
            np.stack([i0["norm_w"], i0["conv1d_b"], i0["dt_proj_b"], i0["D_param"], i0["dw_b"],
                      at["bq"], at["bk"], at["bv"], at["bo"]], 1),
            i0["conv1d_w"], i0["dw_w"].reshape(C, 9), i0["A_log"]], 1),
        "scal": np.stack([i0["scale_mod"], i0["res_scale"]], 1),
        "k128": k128,
        "k32": k32,
        "w_in": i0["in_proj_w"].T,
        "w_x": np.concatenate([xp[RANK:], xp[:RANK]], 0).T,
        "w_dt": i0["dt_proj_w"].T,
        "w_out": i0["out_proj_w"].T,
        "wq": at["Wq"], "wk": at["Wk"], "wv": at["Wv"], "wo": at["Wo"],
        "fc1": ff["c_fc_1"].T, "fc2": ff["c_fc_2"].T, "pr1": ff["c_proj_1"].T, "pr2": ff["c_proj_2"],
    }
    nc = bacc.Bacc("TRN2", target_bir_lowering=False, num_devices=1)
    feed, args = {}, []
    for name, a in arrays.items():
        a = np.ascontiguousarray(a)
        feed[f"in_{name}"] = a
        args.append(nc.dram_tensor(f"in_{name}", a.shape, mybir.dt.from_np(a.dtype), kind="ExternalInput").ap())
    out = nc.dram_tensor("out_x", (NB, C, L), F32, kind="ExternalOutput").ap()
    kept = nc.dram_tensor("kept_residual", (C, L), F32, kind="Internal").ap()
    hybrid_block(nc, *args, kept, out)
    r = run_bass_kernel_spmd(nc, [feed], core_ids=[0])
    return r.results[0]["out_x"].reshape(NB, C, HH, WW)
```
